# Optimizing a Trainium2 kernel written in Bass

```python
import numpy as np
import jax
import jax.numpy as jnp

def _softmax(x, axis=-1):
    return jax.nn.softmax(x, axis=axis)

def _gelu(x):
    return jax.nn.gelu(x, approximate=True)

def _silu(x):
    return jax.nn.silu(x)

def _sigmoid(x):
    return jax.nn.sigmoid(x)

def _layernorm(x, axis=-1, eps=1e-05):
    m = jnp.mean(x, axis=axis, keepdims=True)
    v = jnp.var(x, axis=axis, keepdims=True)
    return (x - m) / jnp.sqrt(v + eps)

def _scatter_add(tgt, idx, src, axis=0):
    return tgt.at[idx].add(src)

def _segment_sum(src, seg, n):
    return jax.ops.segment_sum(src, seg, n)
kernel_name = 'mk_flamingo_gated_d1_seqx_r4_9ecc74'

def setup_inputs(seed: int=0):
    np.random.seed(seed)
    _w = jnp.asarray

    def _rec_inputs():
        import jax
        import jax.numpy as jnp
        _rk = jax.random.key(seed)
        x = -0.0002928 + 1 * jax.random.normal(jax.random.fold_in(_rk, 1), (16, 128, 512), jnp.float32)
        _lenS = 128 - jax.random.randint(jax.random.fold_in(_rk, 7), (16,), 0, max(1, 128 // 4) + 1, jnp.int32)
        _lenS2 = 128 - jax.random.randint(jax.random.fold_in(_rk, 8), (16,), 0, max(1, 128 // 4) + 1, jnp.int32)
        _ctx_2048P = jax.random.normal(jax.random.fold_in(_rk, 11), (16, 16, 512), jnp.float32)
        _ctx_2048c = jax.random.dirichlet(jax.random.fold_in(_rk, 511), 0.3 * jnp.ones((16,), jnp.float32), (16, 128))
        _ctx_2048t = jnp.einsum('bsk,bkd->bsd', _ctx_2048c, _ctx_2048P)
        _ctx_2048t = _ctx_2048t * jax.lax.rsqrt(jnp.mean(jnp.square(_ctx_2048t)) + 1e-12) * 0.953939
        ctx_2048 = -1.39393e-06 + 0.999914 * (_ctx_2048t + 0.3 * jax.random.normal(jax.random.fold_in(_rk, 611), (16, 128, 512), jnp.float32))
        _g = jax.random.normal(jax.random.fold_in(_rk, 9001), (2, 1), jnp.float32)
        _g = jnp.sign(_g) * jnp.maximum(jnp.abs(_g), 1.0) + (_g == 0) * 1.0
        g_xattn = _g[0]
        g_ffn = _g[1]
        return (x, ctx_2048, g_xattn, g_ffn)
    x, ctx_2048, g_xattn, g_ffn = _rec_inputs()

    def _L0_xattn_setup():
        import jax, jax.numpy as jnp
        import numpy as np
        N_HEADS = 8
        ROPE_BASE = 10000.0

        def _rope(x, d):
            t = x.shape[2]
            theta = 1.0 / ROPE_BASE ** (jnp.arange(0, d, 2, dtype=jnp.float32) / d)
            idx = jnp.arange(t, dtype=jnp.float32)[:, None] * theta[None, :]
            idx2 = jnp.concatenate([idx, idx], axis=-1)
            cos = jnp.cos(idx2)[None, None, :, :]
            sin = jnp.sin(idx2)[None, None, :, :]
            x_rope, x_pass = (x[..., :d], x[..., d:])
            d2 = d // 2
            neg_half = jnp.concatenate([-x_rope[..., d2:], x_rope[..., :d2]], axis=-1)
            x_rope = x_rope * cos + neg_half * sin
            return jnp.concatenate([x_rope, x_pass], axis=-1)

        def _proj(W, b, x):
            return jnp.einsum('oc,bct->bot', W, x) + b[None, :, None]
        key = jax.random.key(seed)
        ks = jax.random.split(key, 12)
        B, CH, T = (4, 128, 512)
        s = 1.0 / np.sqrt(CH)
        return {'x': jax.random.normal(ks[0], (B, CH, T), jnp.float32), 'c': jax.random.normal(ks[1], (B, CH, T), jnp.float32), 'Wq': jax.random.normal(ks[2], (CH, CH), jnp.float32) * s, 'bq': jax.random.normal(ks[3], (CH,), jnp.float32) * 0.01, 'Wk': jax.random.normal(ks[4], (CH, CH), jnp.float32) * s, 'bk': jax.random.normal(ks[5], (CH,), jnp.float32) * 0.01, 'Wv': jax.random.normal(ks[6], (CH, CH), jnp.float32) * s, 'bv': jax.random.normal(ks[7], (CH,), jnp.float32) * 0.01, 'Wo': jax.random.normal(ks[8], (CH, CH), jnp.float32) * s, 'bo': jax.random.normal(ks[9], (CH,), jnp.float32) * 0.01}
    _L0_xattn_all = _L0_xattn_setup()
    _L0_xattn_in = {k: v for k, v in _L0_xattn_all.items() if k in ('Wq', 'bq', 'Wk', 'bk', 'Wv', 'bv', 'Wo', 'bo')}
    del _L0_xattn_all

    def _L0_ffn_setup():
        import jax, jax.numpy as jnp
        import numpy as np
        _FP4_LUT = jnp.array([0.0, 0.5, 1.0, 1.5, 2.0, 3.0, 4.0, 6.0, -0.0, -0.5, -1.0, -1.5, -2.0, -3.0, -4.0, -6.0], dtype=jnp.float32)
        GROUP_SIZE = 128
        EPS = 1e-06

        def _dequant_fp4(packed_i32, scales_f16, group_size):
            out_f, in_p = packed_i32.shape
            w = packed_i32.astype(jnp.uint32)
            shifts = jnp.arange(8, dtype=jnp.uint32) * 4
            nib = w[:, :, None] >> shifts & jnp.uint32(15)
            vals = _FP4_LUT[nib.astype(jnp.int32)].reshape(out_f, in_p * 8)
            s = scales_f16.astype(jnp.float32).T
            s_full = jnp.repeat(s, group_size, axis=1)
            return vals * s_full
        key = jax.random.key(seed)
        k1, k2, k3, k4, k5 = jax.random.split(key, 5)
        B, S, H, I = (4, 512, 512, 1408)
        x = jax.random.normal(k1, (B, S, H), dtype=jnp.float32)
        gate_up_packed = jax.random.randint(k2, (2 * I, H // 8), 0, 2147483647, dtype=jnp.int32)
        gate_up_scales = jax.random.uniform(k3, (H // GROUP_SIZE, 2 * I), dtype=jnp.float32).astype(jnp.float16)
        down_packed = jax.random.randint(k4, (H, I // 8), 0, 2147483647, dtype=jnp.int32)
        down_scales = jax.random.uniform(k5, (I // GROUP_SIZE, H), dtype=jnp.float32).astype(jnp.float16)
        return {'x': x, 'gate_up_packed': gate_up_packed, 'gate_up_scales': gate_up_scales, 'down_packed': down_packed, 'down_scales': down_scales}
    _L0_ffn_all = _L0_ffn_setup()
    _L0_ffn_in = {k: v for k, v in _L0_ffn_all.items() if k in ('gate_up_packed', 'gate_up_scales', 'down_packed', 'down_scales')}
    del _L0_ffn_all
    return {'x': x, 'ctx_2048': ctx_2048, 'g_xattn': g_xattn, 'g_ffn': g_ffn, 'L0_xattn_Wq': _L0_xattn_in['Wq'], 'L0_xattn_bq': _L0_xattn_in['bq'], 'L0_xattn_Wk': _L0_xattn_in['Wk'], 'L0_xattn_bk': _L0_xattn_in['bk'], 'L0_xattn_Wv': _L0_xattn_in['Wv'], 'L0_xattn_bv': _L0_xattn_in['bv'], 'L0_xattn_Wo': _L0_xattn_in['Wo'], 'L0_xattn_bo': _L0_xattn_in['bo'], 'L0_ffn_gate_up_packed': _L0_ffn_in['gate_up_packed'], 'L0_ffn_gate_up_scales': _L0_ffn_in['gate_up_scales'], 'L0_ffn_down_packed': _L0_ffn_in['down_packed'], 'L0_ffn_down_scales': _L0_ffn_in['down_scales']}

def reference(x, ctx_2048, g_xattn, g_ffn, L0_xattn_Wq, L0_xattn_bq, L0_xattn_Wk, L0_xattn_bk, L0_xattn_Wv, L0_xattn_bv, L0_xattn_Wo, L0_xattn_bo, L0_ffn_gate_up_packed, L0_ffn_gate_up_scales, L0_ffn_down_packed, L0_ffn_down_scales):
    import jax
    import jax.numpy as jnp

    def _L0_xattn_ref(x, c, Wq, bq, Wk, bk, Wv, bv, Wo, bo):
        import jax, jax.numpy as jnp
        import numpy as np
        N_HEADS = 8
        ROPE_BASE = 10000.0

        def _rope(x, d):
            t = x.shape[2]
            theta = 1.0 / ROPE_BASE ** (jnp.arange(0, d, 2, dtype=jnp.float32) / d)
            idx = jnp.arange(t, dtype=jnp.float32)[:, None] * theta[None, :]
            idx2 = jnp.concatenate([idx, idx], axis=-1)
            cos = jnp.cos(idx2)[None, None, :, :]
            sin = jnp.sin(idx2)[None, None, :, :]
            x_rope, x_pass = (x[..., :d], x[..., d:])
            d2 = d // 2
            neg_half = jnp.concatenate([-x_rope[..., d2:], x_rope[..., :d2]], axis=-1)
            x_rope = x_rope * cos + neg_half * sin
            return jnp.concatenate([x_rope, x_pass], axis=-1)

        def _proj(W, b, x):
            return jnp.einsum('oc,bct->bot', W, x) + b[None, :, None]
        b, ch, t_t = x.shape
        t_s = c.shape[2]
        h = N_HEADS
        kc = ch // h
        d_rope = int(kc * 0.5)
        q = _proj(Wq, bq, x)
        k = _proj(Wk, bk, c)
        v = _proj(Wv, bv, c)
        q = q.reshape(b, h, kc, t_t).transpose(0, 1, 3, 2)
        k = k.reshape(b, h, kc, t_s).transpose(0, 1, 3, 2)
        v = v.reshape(b, h, kc, t_s).transpose(0, 1, 3, 2)
        q = _rope(q, d_rope)
        k = _rope(k, d_rope)
        scores = jnp.einsum('bhqd,bhkd->bhqk', q, k) / jnp.sqrt(jnp.float32(kc))
        p_attn = jax.nn.softmax(scores, axis=-1)
        out = jnp.einsum('bhqk,bhkd->bhqd', p_attn, v)
        out = out.transpose(0, 1, 3, 2).reshape(b, ch, t_t)
        return _proj(Wo, bo, out)

    def _L0_ffn_ref(x, gate_up_packed, gate_up_scales, down_packed, down_scales):
        import jax, jax.numpy as jnp
        import numpy as np
        _FP4_LUT = jnp.array([0.0, 0.5, 1.0, 1.5, 2.0, 3.0, 4.0, 6.0, -0.0, -0.5, -1.0, -1.5, -2.0, -3.0, -4.0, -6.0], dtype=jnp.float32)
        GROUP_SIZE = 128
        EPS = 1e-06

        def _dequant_fp4(packed_i32, scales_f16, group_size):
            out_f, in_p = packed_i32.shape
            w = packed_i32.astype(jnp.uint32)
            shifts = jnp.arange(8, dtype=jnp.uint32) * 4
            nib = w[:, :, None] >> shifts & jnp.uint32(15)
            vals = _FP4_LUT[nib.astype(jnp.int32)].reshape(out_f, in_p * 8)
            s = scales_f16.astype(jnp.float32).T
            s_full = jnp.repeat(s, group_size, axis=1)
            return vals * s_full
        I = gate_up_packed.shape[0] // 2
        w_gu = _dequant_fp4(gate_up_packed, gate_up_scales, GROUP_SIZE)
        w_down = _dequant_fp4(down_packed, down_scales, GROUP_SIZE)
        gate_up = jnp.einsum('bsh,oh->bso', x, w_gu)
        gate, up = (gate_up[..., :I], gate_up[..., I:])
        h = jax.nn.silu(gate) * up
        y = jnp.einsum('bsi,hi->bsh', h, w_down)
        rms = jnp.sqrt(jnp.mean(y * y, axis=-1, keepdims=True) + EPS)
        return y / rms
    x = x + jnp.tanh(g_xattn[0]) * _L0_xattn_ref(_layernorm(x, axis=-1), ctx_2048, L0_xattn_Wq, L0_xattn_bq, L0_xattn_Wk, L0_xattn_bk, L0_xattn_Wv, L0_xattn_bv, L0_xattn_Wo, L0_xattn_bo)
    x = x + jnp.tanh(g_ffn[0]) * _L0_ffn_ref(_layernorm(x, axis=-1), L0_ffn_gate_up_packed, L0_ffn_gate_up_scales, L0_ffn_down_packed, L0_ffn_down_scales)
    return x

_drawn_inputs = setup_inputs


def setup_inputs(seed=0):
    import zlib

    import numpy as np

    out = dict(_drawn_inputs(seed))
    spreads = {}
    factors = {'L0_xattn_bq': 24.867, 'L0_xattn_bk': 52.095, 'L0_xattn_bv': 8.0, 'L0_xattn_bo': 8.0}
    for name, (base, spread) in spreads.items():
        noise = np.random.default_rng([zlib.crc32(name.encode()), seed]).standard_normal(out[name].shape)
        drawn = base * np.exp(spread * noise) if base else spread * noise
        out[name] = jnp.asarray(drawn.astype(out[name].dtype))
    for name, factor in factors.items():
        out[name] = (out[name] * factor).astype(out[name].dtype)
    return out
```

```python
from contextlib import ExitStack

import numpy as np

import concourse.bass as bass
from concourse import mybir

ALU = mybir.AluOpType
ACT = mybir.ActivationFunctionType
AXIS_X = mybir.AxisListType.X
F32 = mybir.dt.float32
F32R = mybir.dt.float32r
BF16 = mybir.dt.bfloat16
F16 = mybir.dt.float16
FP8E3 = mybir.dt.float8e3
U32 = mybir.dt.uint32

P = 128
B = 16
T = 512
HEADS = 8
KC = P // HEADS
ROT = KC // 2
KT = T // P
INNER = 1408
IT = INNER // P
GU = 2 * INNER // P
LN_EPS = 1e-5
RMS_EPS = 1e-6
SCORE_SCALE = KC ** -0.5

STACK = 64
PARTS = 3
MAX_ROW = PARTS * KC
QUAD = 4
GROUP = 4


def unpack_weights(nc, d, keep):
    with ExitStack() as ctx:
        sb = lambda name, shape, dt: ctx.enter_context(nc.sbuf_tensor(name, shape, dt))
        ps = lambda name, shape, dt: ctx.enter_context(nc.psum_tensor(name, shape, dt))
        sem = lambda name: ctx.enter_context(nc.semaphore(name))
        gu_words, dn_words = GU * T // 8, KT * INNER // 8
        words = gu_words + dn_words
        packed = sb("packed", [P, words], U32)
        part_a = sb("part_a", [P, words], U32)
        part_b = sb("part_b", [P, words], U32)
        sign = sb("sign", [P, words], U32)
        gu_vals = sb("gu_vals", [P, GU, 2, T // 2], BF16)
        dn_vals = sb("dn_vals", [P, KT, 2, INNER // 2], BF16)
        gu_sc16 = sb("gu_sc16", [KT * GU, P], F16)
        dn_sc16 = sb("dn_sc16", [IT * KT, P], F16)
        gu_sc32 = sb("gu_sc32", [KT * GU, P], F32)
        dn_sc32 = sb("dn_sc32", [IT * KT, P], F32)
        gu_sc = sb("gu_sc", [P, KT, GU], F32)
        dn_sc = sb("dn_sc", [P, IT, KT], F32)
        wtile = [sb(f"wtile{p}", [P, T], F32) for p in range(2)]
        wt_ps = [ps(f"wt_ps{p}", [P, KT, P], F32) for p in range(2)]
        sc_ps = ps("sc_ps", [P, KT * GU + IT * KT], F32)

        packed_in = sem("packed_in")
        scales_in = sem("scales_in")
        ident_in = sem("ident_in")
        bits = sem("bits")
        scales_f32 = sem("scales_f32")
        scales_t = sem("scales_t")
        scales_ok = sem("scales_ok")
        vals_ok = sem("vals_ok")
        scaled = sem("scaled")
        turned = sem("turned")
        heads = sem("heads")
        rests = sem("rests")
        chunks = [(t, g0, min(KT, IT - g0)) for t in range(KT) for g0 in range(0, IT, KT)]

        with nc.Block() as block:
            @block.sync
            def _(sp):
                sp.dma_start(packed[:, 0:gu_words].rearrange("p (t w) -> p t w", t=GU),
                             d["gate_up_packed"].rearrange("(t p) w -> p t w", p=P)).then_inc(packed_in, 16)
                sp.dma_start(packed[:, gu_words:words].rearrange("p (t w) -> p t w", t=KT),
                             d["down_packed"].rearrange("(t p) w -> p t w", p=P)).then_inc(packed_in, 16)
                sp.dma_start(gu_sc16[:], d["gate_up_scales"].rearrange("g (t o) -> (g t) o", o=P)).then_inc(scales_in, 16)
                sp.dma_start(dn_sc16[:], d["down_scales"].rearrange("g (t o) -> (g t) o", o=P)).then_inc(scales_in, 16)
                sp.dma_start(keep["ident"][:], d["ident"]).then_inc(ident_in, 16)

            @block.vector
            def _(dve):
                dve.wait_ge(packed_in, 32)
                nc.vector.tensor_scalar(part_a[:], packed[:], 0x07070707, 3, ALU.bitwise_and,
                                        ALU.logical_shift_left).then_inc(bits, 1)
                nc.vector.tensor_scalar(sign[:], packed[:], 0x08080808, 4, ALU.bitwise_and,
                                        ALU.logical_shift_left).then_inc(bits, 1)
                nc.vector.tensor_scalar(part_b[:], packed[:], 0x70707070, 1, ALU.bitwise_and,
                                        ALU.logical_shift_right).then_inc(bits, 1)
                dve.wait_ge(bits, 3)
                nc.vector.tensor_tensor(part_a[:], part_a[:], sign[:], ALU.bitwise_or).then_inc(bits, 1)
                nc.vector.tensor_scalar(packed[:], packed[:], 0x80808080, None, ALU.bitwise_and).then_inc(bits, 1)
                dve.wait_ge(bits, 5)
                nc.vector.tensor_tensor(part_b[:], part_b[:], packed[:], ALU.bitwise_or).then_inc(bits, 1)

                dve.wait_ge(scales_ok, 2)

                def scale_tile(buf, vals, scales, groups):
                    for odd in range(2):
                        out = buf[:, 0:groups * P].rearrange("p (g c two) -> p g c two", g=groups, two=2)[:, :, :, odd]
                        last = nc.vector.tensor_tensor(
                            out, vals[odd].rearrange("p (g c) -> p g c", g=groups),
                            scales.unsqueeze(2).to_broadcast([P, groups, P // 2]), ALU.mult)
                    last.then_inc(scaled, 1)

                def rest_tile(rest, head, tile_ps):
                    nc.vector.tensor_tensor(rest, tile_ps, head.bitcast(F32), ALU.subtract).then_inc(rests, 1)

                dve.wait_ge(vals_ok, 4)
                with dve.Fori(0, GU // 2) as i:
                    for p in range(2):
                        t = i * 2 + p
                        scale_tile(wtile[p], [gu_vals[:, bass.ds(t, 1), o, :].rearrange("p a c -> p (a c)") for o in range(2)],
                                   gu_sc[:, :, bass.ds(t, 1)].rearrange("p g a -> p (g a)"), KT)
                        dve.wait_ge(heads, t + 1)
                        rest_tile(keep["gu_rest"][:, :, bass.ds(t * P, P)], keep["gu_head"][:, :, bass.ds(t * P, P)],
                                  wt_ps[p][:])
                for n, (t, g0, groups) in enumerate(chunks):
                    p, at = n % 2, GU + n
                    scale_tile(wtile[p], [dn_vals[:, t, o, g0 * 64:(g0 + groups) * 64] for o in range(2)],
                               dn_sc[:, g0:g0 + groups, t], groups)
                    dve.wait_ge(heads, at + 1)
                    rest_tile(keep["dn_rest"][:, g0:g0 + groups, t * P:(t + 1) * P],
                              keep["dn_head"][:, g0:g0 + groups, t * P:(t + 1) * P], wt_ps[p][:, 0:groups, :])

            @block.scalar
            def _(act):
                act.wait_ge(scales_in, 32)
                nc.scalar.activation(gu_sc32[:], gu_sc16[:], ACT.Copy, scale=4.0).then_inc(scales_f32, 1)
                nc.scalar.activation(dn_sc32[:], dn_sc16[:], ACT.Copy, scale=4.0).then_inc(scales_f32, 1)
                act.wait_ge(scales_t, 2)
                nc.scalar.activation(gu_sc[:].rearrange("p g t -> p (g t)"), sc_ps[:, 0:KT * GU], ACT.Copy).then_inc(scales_ok, 1)
                nc.scalar.activation(dn_sc[:].rearrange("p g t -> p (g t)"), sc_ps[:, KT * GU:], ACT.Copy).then_inc(scales_ok, 1)
                for odd, part, need in ((0, part_a, 4), (1, part_b, 6)):
                    act.wait_ge(bits, need)
                    by = part[:].bitcast(FP8E3)
                    nc.scalar.activation(gu_vals[:, :, odd, :], by[:, 0:4 * gu_words].rearrange("p (t c) -> p t c", t=GU),
                                         ACT.Copy).then_inc(vals_ok, 1)
                    nc.scalar.activation(dn_vals[:, :, odd, :], by[:, 4 * gu_words:].rearrange("p (t c) -> p t c", t=KT),
                                         ACT.Copy).then_inc(vals_ok, 1)
                with act.Fori(0, GU // 2) as i:
                    for p in range(2):
                        t = i * 2 + p
                        act.wait_ge(turned, t + 1)
                        nc.scalar.activation(keep["gu_head"][:, :, bass.ds(t * P, P)], wt_ps[p][:], ACT.Copy).then_inc(heads, 1)
                for n, (t, g0, groups) in enumerate(chunks):
                    act.wait_ge(turned, GU + n + 1)
                    nc.scalar.activation(keep["dn_head"][:, g0:g0 + groups, t * P:(t + 1) * P],
                                         wt_ps[n % 2][:, 0:groups, :], ACT.Copy).then_inc(heads, 1)

            @block.tensor
            def _(pe):
                pe.wait_ge(ident_in, 16)
                pe.wait_ge(scales_f32, 2)
                nc.tensor.transpose(sc_ps[:, 0:KT * GU], gu_sc32[:], keep["ident"][0:KT * GU, 0:KT * GU]).then_inc(scales_t, 1)
                nc.tensor.transpose(sc_ps[:, KT * GU:], dn_sc32[:], keep["ident"][0:IT * KT, 0:IT * KT]).then_inc(scales_t, 1)

                def turn(p, groups):
                    for k in range(groups):
                        last = nc.tensor.transpose(wt_ps[p][:, k, :], wtile[p][:, k * P:(k + 1) * P], keep["ident"][:])
                    last.then_inc(turned, 1)

                with pe.Fori(0, GU // 2) as i:
                    for p in range(2):
                        pe.wait_ge(scaled, i * 2 + p + 1)
                        turn(p, KT)
                for n, (t, g0, groups) in enumerate(chunks):
                    pe.wait_ge(scaled, GU + n + 1)
                    turn(n % 2, groups)


def project(nc, d, keep):
    with ExitStack() as ctx:
        sb = lambda name, shape, dt: ctx.enter_context(nc.sbuf_tensor(name, shape, dt))
        ps = lambda name, shape, dt: ctx.enter_context(nc.psum_tensor(name, shape, dt))
        sem = lambda name: ctx.enter_context(nc.semaphore(name))
        wq, wk, wv = (sb(n, [P, P], F32) for n in ("wq", "wk", "wv"))
        bias_q, bias_qs, bias_k = (sb(n, [P, 1], F32) for n in ("bias_q", "bias_qs", "bias_k"))
        bias_v = sb("bias_v", [P, P], F32)
        eps = sb("ln_eps", [P, 1], F32)
        cos, sin = sb("cos", [P, T], F32), sb("sin", [P, T], F32)
        two = range(2)
        xt = [sb(f"xt{p}", [P, T], F32) for p in two]
        ct = [sb(f"ct{p}", [P, T], F32) for p in two]
        xn = [sb(f"xn{p}", [P, T], F32) for p in two]
        stats = [sb(f"stats{p}", [P, 6], F32) for p in two]
        moments = [sb(f"moments{p}", [P, 2], F32) for p in two]
        rstd = [sb(f"rstd{p}", [P, 2], F32) for p in two]
        proj = [sb(f"proj{p}", [P, 2, T], F32) for p in two]
        swap = [sb(f"swap{p}", [P, 2, T], F32) for p in two]
        by_cos = [sb(f"by_cos{p}", [P, 2, T], F32) for p in two]
        split = [sb(f"split{p}", [P, 2, 2, T], F32R) for p in two]
        vt = [sb(f"vt{p}", [P, T], F32) for p in two]
        q_ps = [ps(f"q_ps{p}", [P, T], F32) for p in two]
        k_ps = [ps(f"k_ps{p}", [P, T], F32) for p in two]
        v_ps = [ps(f"v_ps{p}", [P, T], F32) for p in two]

        const_in = sem("const_in")
        loaded = [sem(f"loaded{p}") for p in two]
        stored = [sem(f"stored{p}") for p in two]
        consts = sem("consts")
        stat = sem("stat")
        dev = sem("dev")
        inv = sem("inv")
        normed = sem("normed")
        projected = sem("projected")
        biased = sem("biased")
        swapped = sem("swapped")
        cosine = sem("cosine")
        rotated = sem("rotated")
        heads = sem("heads1")
        rests = sem("rests1")
        passed = sem("passed1")
        v_ready = sem("v_ready")
        partner = [(i // KC) * KC + ((i % KC + ROT // 2) % ROT if i % KC < ROT else i % KC) for i in range(32)]

        with nc.Block() as block:
            @block.sync
            def _(sp):
                for out, name in ((wq, "wqT"), (wk, "wkT"), (wv, "wvT"), (cos, "cos"), (sin, "sin")):
                    sp.dma_start(out[:], d[name]).then_inc(const_in, 16)
                sp.dma_start(bias_q[:], d["bq"].rearrange("(p a) -> p a", a=1)).then_inc(const_in, 16)
                sp.dma_start(bias_k[:], d["bk"].rearrange("(p a) -> p a", a=1)).then_inc(const_in, 16)
                sp.dma_start(bias_v[:], d["bv"].rearrange("(a n) -> a n", a=1).to_broadcast([P, P])).then_inc(const_in, 16)

                def load(b, p):
                    sp.dma_start(xt[p][:], d["x"][bass.ds(b, 1)].rearrange("a p t -> (a p) t")).then_inc(loaded[p], 16)
                    sp.dma_start(ct[p][:], d["ctx"][bass.ds(b, 1)].rearrange("a p t -> (a p) t")).then_inc(loaded[p], 16)

                def store(b, p):
                    sp.dma_start(keep["qk_dram"][bass.ds(b, 1)].rearrange("a w s p t -> p (a w s) t"),
                                 split[p][:].bitcast(F32).rearrange("p w s t -> p (w s) t")).then_inc(stored[p], 16)
                    sp.dma_start(keep["v_dram"][bass.ds(b, 1)].rearrange("a p t -> (a p) t"), vt[p][:]).then_inc(stored[p], 16)

                for p in two:
                    load(p, p)
                with sp.Fori(0, B // 2 - 1) as i:
                    for p in two:
                        b = i * 2 + p
                        sp.wait_ge(projected, b + 1)
                        load(b + 2, p)
                        sp.wait_ge(rests, 2 * b + 2)
                        sp.wait_ge(v_ready, b + 1)
                        store(b, p)
                for p in two:
                    b = B - 2 + p
                    sp.wait_ge(rests, 2 * b + 2)
                    sp.wait_ge(v_ready, b + 1)
                    store(b, p)
                for p in two:
                    sp.wait_ge(stored[p], 32 * (B // 2))

            def vector_step(dve, i, p, first):
                b = i * 2 + p
                dve.wait_ge(loaded[p], i * 32 + 32)
                nc.vector.bn_stats(stats[p][:], xt[p][:]).then_inc(stat, 1)
                dve.wait_ge(stat, b * 2 + 1)
                dve.sem_inc(passed, 1)
                nc.vector.bn_aggr(moments[p][:], stats[p][:]).then_inc(stat, 1)
                dve.wait_ge(dev, b + 1)
                nc.vector.reciprocal(rstd[p][:, 1:2], rstd[p][:, 0:1]).then_inc(inv, 1)
                dve.wait_ge(inv, b + 1)
                nc.vector.tensor_scalar(xn[p][:], xt[p][:], moments[p][:, 0:1], rstd[p][:, 1:2], ALU.subtract,
                                        ALU.mult).then_inc(normed, 1)

            def vector_rotate(dve, i, p, first):
                b = i * 2 + p
                for w in two:
                    dve.wait_ge(biased, b * 2 + w + 1)
                    if not first:
                        dve.wait_ge(rests, b * 2 - 4 + w + 1)
                    dve.sem_inc(passed, 1)
                    nc.vector.stream_shuffle(swap[p][:, w], proj[p][:, w], partner).then_inc(swapped, 1)
                    dve.wait_ge(swapped, b * 4 + 2 * w + 1)
                    nc.vector.tensor_tensor(swap[p][:, w], swap[p][:, w], sin[:], ALU.mult).then_inc(swapped, 1)
                dve.wait_ge(projected, b + 1)
                if not first:
                    dve.wait_ge(stored[p], i * 32)
                nc.vector.tensor_tensor(vt[p][:].rearrange("p (k c) -> p k c", k=KT),
                                        v_ps[p][:].rearrange("p (k c) -> p k c", k=KT),
                                        bias_v[:].unsqueeze(1).to_broadcast([P, KT, P]), ALU.add).then_inc(v_ready, 1)
                for w in two:
                    dve.wait_ge(swapped, b * 4 + 2 * w + 2)
                    dve.wait_ge(cosine, b * 2 + w + 1)
                    nc.vector.tensor_tensor(swap[p][:, w], swap[p][:, w], by_cos[p][:, w], ALU.add).then_inc(rotated, 1)

            @block.vector
            def _(dve):
                dve.wait_ge(const_in, 16 * 8)
                nc.vector.tensor_scalar(bias_qs[:], bias_q[:], SCORE_SCALE, None, ALU.mult).then_inc(consts, 1)
                nc.vector.memset(eps[:], LN_EPS).then_inc(consts, 1)
                vector_step(dve, 0, 0, True)
                vector_step(dve, 0, 1, True)
                vector_rotate(dve, 0, 0, True)
                vector_step(dve, 1, 0, False)
                vector_rotate(dve, 0, 1, True)
                vector_step(dve, 1, 1, False)
                with dve.Fori(1, B // 2 - 1) as i:
                    for p in two:
                        vector_rotate(dve, i, p, False)
                        vector_step(dve, i + 1, p, False)
                for p in two:
                    vector_rotate(dve, B // 2 - 1, p, False)

            def scalar_dev(act, i, p):
                b = i * 2 + p
                act.wait_ge(stat, b * 2 + 2)
                nc.scalar.activation(rstd[p][:, 0:1], moments[p][:, 1:2], ACT.Sqrt, bias=eps[:]).then_inc(dev, 1)

            def scalar_split(act, i, p, first):
                b = i * 2 + p
                act.wait_ge(projected, b + 1)
                if not first:
                    act.wait_ge(cosine, b * 2 - 2)
                nc.scalar.activation(proj[p][:, 0], q_ps[p][:], ACT.Identity, bias=bias_qs[:], scale=SCORE_SCALE).then_inc(biased, 1)
                nc.scalar.activation(proj[p][:, 1], k_ps[p][:], ACT.Identity, bias=bias_k[:]).then_inc(biased, 1)
                for w in two:
                    act.wait_ge(rotated, b * 2 + w + 1)
                    if not first:
                        act.wait_ge(stored[p], i * 32)
                    nc.scalar.activation(split[p][:, w, 0], swap[p][:, w], ACT.Copy).then_inc(heads, 1)

            @block.scalar
            def _(act):
                act.wait_ge(consts, 2)
                scalar_dev(act, 0, 0)
                scalar_dev(act, 0, 1)
                scalar_split(act, 0, 0, True)
                scalar_dev(act, 1, 0)
                scalar_split(act, 0, 1, True)
                scalar_dev(act, 1, 1)
                with act.Fori(1, B // 2 - 1) as i:
                    for p in two:
                        scalar_split(act, i, p, False)
                        scalar_dev(act, i + 1, p)
                for p in two:
                    scalar_split(act, B // 2 - 1, p, False)

            def pool_step(pool, i, p, first):
                b = i * 2 + p
                for w in two:
                    pool.wait_ge(biased, b * 2 + w + 1)
                    nc.gpsimd.tensor_tensor(by_cos[p][:, w], proj[p][:, w], cos[:], ALU.mult).then_inc(cosine, 1)
                for w in two:
                    pool.wait_ge(heads, b * 2 + w + 1)
                    if not first:
                        pool.wait_ge(stored[p], i * 32)
                    nc.gpsimd.tensor_tensor(split[p][:, w, 1], swap[p][:, w], split[p][:, w, 0].bitcast(F32),
                                            ALU.subtract).then_inc(rests, 1)

            @block.gpsimd
            def _(pool):
                pool.wait_ge(const_in, 16 * 8)
                for p in two:
                    pool_step(pool, 0, p, True)
                with pool.Fori(1, B // 2) as i:
                    for p in two:
                        pool_step(pool, i, p, False)

            def tensor_step(pe, i, p, first):
                b = i * 2 + p
                pe.wait_ge(normed, b + 1)
                pe.wait_ge(loaded[p], i * 32 + 32)
                if not first:
                    pe.wait_ge(biased, b * 2 - 2)
                    pe.wait_ge(v_ready, b - 1)
                nc.tensor.matmul(q_ps[p][:], wq[:], xn[p][:], start=True, stop=True)
                nc.tensor.matmul(k_ps[p][:], wk[:], ct[p][:], start=True, stop=True)
                for k in range(KT):
                    last = nc.tensor.matmul(v_ps[p][:, k * P:(k + 1) * P], ct[p][:, k * P:(k + 1) * P], wv[:],
                                            start=True, stop=True)
                last.then_inc(projected, 1)

            @block.tensor
            def _(pe):
                pe.wait_ge(const_in, 16 * 8)
                for p in two:
                    tensor_step(pe, 0, p, True)
                with pe.Fori(1, B // 2) as i:
                    for p in two:
                        tensor_step(pe, i, p, False)


UNITS = 4
SCORE_UNITS = 3
TILES = HEADS * KT
HALF_LOADS = 2 * 2 * PARTS


def score_tiles(unit, slot):
    if unit >= SCORE_UNITS:
        return []
    n, slots = unit * QUAD + slot, SCORE_UNITS * QUAD
    return [(t // KT, t % KT, t) for t in range(TILES * n // slots, TILES * (n + 1) // slots)]


def attend(nc, d, keep):
    with ExitStack() as ctx:
        sb = lambda name, shape, dt: ctx.enter_context(nc.sbuf_tensor(name, shape, dt))
        ps = lambda name, shape, dt: ctx.enter_context(nc.psum_tensor(name, shape, dt))
        sem = lambda name: ctx.enter_context(nc.semaphore(name))
        two = range(2)
        q_stack = [sb(f"q_stack{p}", [P, HEADS // 2, T], F32R) for p in two]
        k_stack = [sb(f"k_stack{p}", [P, HEADS // 2, T], F32R) for p in two]
        v_in = [sb(f"v_in{p}", [P, KT, HEADS, KC], F32) for p in two]
        v_ones = [sb(f"v_ones{p}", [P, KT, HEADS, 2 * KC], F32) for p in two]
        x_in = [sb(f"x_in{p}", [P, T], F32) for p in two]
        x_out = [sb(f"x_out{p}", [P, T], F32) for p in two]
        probs = [sb(f"probs{p}", [P, QUAD, 2, T], F32) for p in two]
        row_max = [sb(f"row_max{p}", [P, 2, HEADS // 2, KT], F32) for p in two]
        neg_max = [sb(f"neg_max{p}", [2 * HEADS // 2 * KT, P], F32R) for p in two]
        sums_of = sb("pv_sb", [P, T], F32)
        scale_of = sb("scale_of", [P, T], F32)
        heads_out = [sb(f"heads_out{q}", [P, T], F32) for q in two]
        attn = sb("attn", [P, T], F32)
        wo = [sb(f"wo{q}", [P, P], F32) for q in two]
        bias_o, gate_bias = sb("bias_o", [P, 1], F32), sb("gate_bias", [P, 1], F32)
        gate_in = sb("gate_in", [P, 2], F32)

        st_ps = [ps(f"st_ps{p}", [P, 2, T], F32) for p in two]
        s_ps = [ps(f"s_ps{p}", [P, T], F32) for p in two]
        pv_ps = ps("pv_ps", [P, T], F32)
        misc_ps = ps("misc_ps", [P, T], F32)

        const_in = sem("const2_in")
        blank = sem("blank")
        gated = sem("gated")
        half_in = [[sem(f"half_in{p}{h}") for h in two] for p in two]
        vx_in = [sem(f"vx_in{p}") for p in two]
        v_set = sem("v_set")
        scored = sem("scored")
        maxed = sem("maxed")
        max_turned = sem("max_turned")
        max_neg = sem("max_neg")
        max_in = [sem(f"max_in{p}") for p in two]
        st_done = sem("st_done")
        expd = sem("expd")
        pv_done = sem("pv_done")
        pv_out = sem("pv_out")
        passed = sem("passed2")
        pool_passed = sem("pool_passed")
        sums_up = sem("sums_up")
        logs = sem("logs")
        inverses = sem("inverses")
        quad_done = sem("quad_done")
        mixed = sem("mixed")
        attn_ok = sem("attn_ok")
        x_ok = sem("x_ok")
        x_stored = [sem(f"x_stored{p}") for p in two]
        spread = [KC + i % KC for i in range(32)]
        max_rows = HEADS // 2 * KT

        with nc.Block() as block:
            def load_half(sp, b, p, h):
                slots = slice(2 * h, 2 * h + 2)
                for stack, which, parts in ((q_stack, 0, (0, 0, 1)), (k_stack, 1, (0, 1, 0))):
                    for odd in two:
                        for c, part in enumerate(parts):
                            src = keep["qk_dram"][bass.ds(b, 1), which, part].rearrange(
                                "a (j two c) t -> (a two) c j t", two=2, c=KC)[odd, :, slots, :]
                            at = STACK * odd + KC * c
                            sp.dma_start(stack[p][at:at + KC, slots, :].bitcast(F32), src).then_inc(half_in[p][h], 16)

            def load_vx(sp, b, p):
                sp.dma_start(v_in[p][:].rearrange("p k h c -> p (k h c)"),
                             keep["v_dram"][bass.ds(b, 1)].rearrange("a p t -> (a p) t")).then_inc(vx_in[p], 16)
                sp.dma_start(x_in[p][:], d["x"][bass.ds(b, 1)].rearrange("a p t -> (a p) t")).then_inc(vx_in[p], 16)

            def load_max(sp, b, p):
                sp.wait_ge(max_neg, b + 1)
                for odd in two:
                    row = STACK * odd + MAX_ROW
                    sp.dma_start(q_stack[p][row:row + 1, :, :].bitcast(F32).rearrange("a j t -> a (j t)"),
                                 neg_max[p][odd * max_rows:(odd + 1) * max_rows, :].bitcast(F32)).then_inc(max_in[p], 16)

            def store_x(sp, b, p):
                sp.wait_ge(x_ok, b + 1)
                sp.dma_start(keep["x_dram"][bass.ds(b, 1)].rearrange("a p t -> (a p) t"), x_out[p][:]).then_inc(x_stored[p], 16)

            def sync_step(sp, b, p, first, last):
                if not first:
                    sp.wait_ge(st_done, b * 16)
                    if not last:
                        load_half(sp, b + 1, 1 - p, 1)
                if not last and not first:
                    sp.wait_ge(v_set, b)
                    sp.wait_ge(x_ok, b)
                    store_x(sp, b - 1, 1 - p)
                    load_vx(sp, b + 1, 1 - p)
                elif last:
                    store_x(sp, b - 1, 1 - p)

            def sync_late(sp, b, p, ahead):
                if ahead:
                    sp.wait_ge(st_done, b * 16 + 8)
                    load_half(sp, b + 2, p, 0)

            @block.sync
            def _(sp):
                sp.wait_ge(blank, 6)
                for q in two:
                    for j in range(QUAD):
                        rows = slice((q * QUAD + j) * KC, (q * QUAD + j + 1) * KC)
                        sp.dma_start(wo[q][2 * KC * j:2 * KC * j + KC, :], d["woT"][rows, :]).then_inc(const_in, 16)
                sp.dma_start(bias_o[:], d["bo"].rearrange("(p a) -> p a", a=1)).then_inc(const_in, 16)
                sp.dma_start(gate_in[:, 0:1], d["g_xattn"].rearrange("(a n) -> a n", a=1).to_broadcast([P, 1])).then_inc(const_in, 16)
                sp.dma_start(gate_in[:, 1:2], d["g_ffn"].rearrange("(a n) -> a n", a=1).to_broadcast([P, 1])).then_inc(const_in, 16)
                for b in two:
                    load_half(sp, b, b, 0)
                    load_half(sp, b, b, 1)
                    load_vx(sp, b, b)
                load_max(sp, 0, 0)
                sync_step(sp, 0, 0, True, False)
                sync_late(sp, 0, 0, True)
                load_max(sp, 1, 1)
                sync_step(sp, 1, 1, False, False)
                sync_late(sp, 1, 1, True)
                load_max(sp, 2, 0)
                with sp.Fori(1, B // 2 - 1) as i:
                    for p in two:
                        b = i * 2 + p
                        sync_step(sp, b, p, False, False)
                        sync_late(sp, b, p, True)
                        load_max(sp, b + 1, 1 - p)
                sync_step(sp, B - 2, 0, False, False)
                load_max(sp, B - 1, 1)
                sync_step(sp, B - 1, 1, False, True)
                store_x(sp, B - 1, 1)
                for p in two:
                    sp.wait_ge(x_stored[p], 16 * (B // 2))

            def score(pe, b, p, tiles):
                for head, qt, n in tiles:
                    rows = slice(STACK * (head % 2), STACK * (head % 2) + MAX_ROW)
                    at = b * TILES + n
                    if n == 0:
                        pe.wait_ge(half_in[p][0], (b // 2 if isinstance(b, int) else (b - p) // 2) * 16 * HALF_LOADS + 16 * HALF_LOADS)
                    if n == TILES // 2:
                        pe.wait_ge(half_in[p][1], (b // 2 if isinstance(b, int) else (b - p) // 2) * 16 * HALF_LOADS + 16 * HALF_LOADS)
                    if not (isinstance(b, int) and at < 2):
                        pe.wait_ge(maxed, at - 1)
                    nc.tensor.matmul(s_ps[n % 2][:], q_stack[p][rows, head // 2, qt * P:(qt + 1) * P],
                                     k_stack[p][rows, head // 2, :], start=True, stop=True).then_inc(scored, 1)

            def turn_max(pe, b, p, first):
                pe.wait_ge(maxed, b * TILES + TILES)
                if not first:
                    pe.wait_ge(attn_ok, b - 1)
                nc.tensor.transpose(misc_ps[0:2 * max_rows, 0:P], row_max[p][:].rearrange("p a j k -> p (a j k)"),
                                    keep["ident"][:]).then_inc(max_turned, 1)

            def values(pe, unit, b, p, half, k):
                quad = half // 2
                at = b * UNITS + half
                if k == 0:
                    pe.wait_ge(expd, at * QUAD + QUAD)
                    if half == 0:
                        pe.wait_ge(v_set, b + 1)
                    if half % 2 == 0 and not (isinstance(b, int) and b == 0 and quad == 0):
                        pe.wait_ge(pv_out, b * 2 + quad)
                for j in range(QUAD):
                    kt = 2 * (half % 2) + k
                    rows = slice(2 * KC * j, 2 * KC * (j + 1))
                    last = nc.tensor.matmul(pv_ps[rows, :], v_ones[p][:, kt, quad * QUAD + j, :], probs[half % 2][:, j, k, :],
                                            start=(kt == 0), stop=(kt == KT - 1))
                if k == 1:
                    last.then_inc(pv_done, 1)

            def mix(pe, b, p):
                pe.wait_ge(quad_done, b * 2 + 2)
                pe.wait_ge(max_neg, b + 2 if not (isinstance(b, int) and b == B - 1) else B)
                for q in two:
                    last = nc.tensor.matmul(misc_ps[:], wo[q][:], heads_out[q][:], start=(q == 0), stop=(q == 1))
                last.then_inc(mixed, 1)

            def tensor_step(pe, b, p, first, last):
                for unit in range(UNITS):
                    for slot in range(QUAD):
                        at = b * 16 + unit * QUAD + slot
                        if unit == 0 and slot == 0:
                            pe.wait_ge(max_in[p], (b // 2 if isinstance(b, int) else (b - p) // 2) * 32 + 32)
                        if not (first and unit == 0 and slot < 2):
                            pe.wait_ge(expd, at - 1)
                        head = (unit // 2) * QUAD + slot
                        rows = slice(STACK * (head % 2), STACK * (head % 2) + MAX_ROW + 1)
                        for k in range(2):
                            kt = 2 * (unit % 2) + k
                            mm = nc.tensor.matmul(st_ps[slot % 2][:, k, :], k_stack[p][rows, head // 2, kt * P:(kt + 1) * P],
                                                  q_stack[p][rows, head // 2, :], start=True, stop=True)
                        mm.then_inc(st_done, 1)
                        if not last:
                            score(pe, b + 1, 1 - p, score_tiles(unit, slot))
                            if unit == SCORE_UNITS and slot == 0:
                                turn_max(pe, b + 1, 1 - p, first)
                        if slot % 2 and not (first and unit == 0):
                            if unit:
                                values(pe, unit, b, p, unit - 1, slot // 2)
                            else:
                                values(pe, unit, b - 1, 1 - p, UNITS - 1, slot // 2)
                        if unit == 2 and slot == 2 and not first:
                            mix(pe, b - 1, 1 - p)

            @block.tensor
            def _(pe):
                pe.wait_ge(const_in, 16 * 11)
                score(pe, 0, 0, [(t // KT, t % KT, t) for t in range(TILES)])
                turn_max(pe, 0, 0, True)
                tensor_step(pe, 0, 0, True, False)
                tensor_step(pe, 1, 1, False, False)
                with pe.Fori(1, B // 2 - 1) as i:
                    for p in two:
                        tensor_step(pe, i * 2 + p, p, False, False)
                tensor_step(pe, B - 2, 0, False, False)
                tensor_step(pe, B - 1, 1, False, True)
                for k in two:
                    values(pe, 0, B - 1, 1, UNITS - 1, k)
                mix(pe, B - 1, 1)

            def quad_out(act, b, quad):
                act.wait_ge(pv_done, b * UNITS + 2 * quad + 2)
                if not (isinstance(b, int) and b == 0 and quad == 0):
                    act.wait_ge(quad_done, b * 2 + quad)
                nc.scalar.activation(sums_of[:], pv_ps[:], ACT.Copy).then_inc(pv_out, 1)

            def quad_inverse(act, b, quad):
                act.wait_ge(sums_up, b * 2 + quad + 1)
                nc.scalar.activation(scale_of[:], scale_of[:], ACT.Ln).then_inc(logs, 1)
                act.wait_ge(logs, b * 2 + quad + 1)
                nc.scalar.activation(scale_of[:], scale_of[:], ACT.Exp, scale=-1.0).then_inc(inverses, 1)

            def gate(act, b):
                act.wait_ge(mixed, b + 1)
                if not (isinstance(b, int) and b == 0):
                    act.wait_ge(x_ok, b)
                nc.scalar.activation(attn[:], misc_ps[:], ACT.Identity, bias=gate_bias[:], scale=keep["gates"][:, 0:1]).then_inc(attn_ok, 1)

            def scalar_step(act, b, p, first):
                for unit in range(UNITS):
                    done = (b - 1, 1) if unit == 1 else (b, 0)
                    for slot in range(QUAD):
                        if slot == 0 and unit % 2 and not (first and unit == 1):
                            quad_out(act, *done)
                        at = b * 16 + unit * QUAD + slot
                        act.wait_ge(st_done, at + 1)
                        if slot == 0 and not (first and unit < 2):
                            act.wait_ge(pv_done, b * UNITS + unit - 1)
                        nc.scalar.activation(probs[unit % 2][:, slot], st_ps[slot % 2][:], ACT.Exp).then_inc(expd, 1)
                        if slot == 2 and unit % 2 and not (first and unit == 1):
                            quad_inverse(act, *done)
                        if slot == 0 and unit == 3 and not first:
                            gate(act, b - 1)

            @block.scalar
            def _(act):
                act.wait_ge(const_in, 16 * 11)
                nc.scalar.activation(keep["gates"][:], gate_in[:], ACT.Tanh).then_inc(gated, 1)
                nc.scalar.preload_act_table(ACT.Ln)
                act.wait_ge(blank, 7)
                scalar_step(act, 0, 0, True)
                scalar_step(act, 1, 1, False)
                with act.Fori(1, B // 2) as i:
                    for p in two:
                        scalar_step(act, i * 2 + p, p, False)
                quad_out(act, B - 1, 1)
                quad_inverse(act, B - 1, 1)
                gate(act, B - 1)

            def maxima(dve, b, p, tiles):
                for head, qt, n in tiles:
                    dve.wait_ge(scored, b * TILES + n + 1)
                    if n == 0 and not (isinstance(b, int) and b < 2):
                        dve.wait_ge(max_turned, b - 1)
                    nc.vector.tensor_reduce(row_max[p][:, head % 2, head // 2, qt:qt + 1], s_ps[n % 2][:], AXIS_X,
                                            ALU.max).then_inc(maxed, 1)

            def negate(dve, b, p):
                dve.wait_ge(max_turned, b + 1)
                if not (isinstance(b, int) and b < 2):
                    dve.wait_ge(max_in[p], (b // 2 if isinstance(b, int) else (b - p) // 2) * 32)
                nc.vector.tensor_scalar(neg_max[p][:], misc_ps[0:2 * max_rows, 0:P], -1.0, None, ALU.mult).then_inc(max_neg, 1)

            def quad_sums(dve, b, quad):
                dve.wait_ge(pv_out, b * 2 + quad + 1)
                dve.sem_inc(passed, 1)
                nc.vector.stream_shuffle(scale_of[:], sums_of[:], spread).then_inc(sums_up, 1)

            def quad_scale(dve, b, quad):
                dve.wait_ge(inverses, b * 2 + quad + 1)
                if not (isinstance(b, int) and b == 0):
                    dve.wait_ge(mixed, b)
                nc.vector.tensor_tensor(heads_out[quad][:], sums_of[:], scale_of[:], ALU.mult).then_inc(quad_done, 1)

            def vector_step(dve, b, p, first, last):
                for unit in range(UNITS):
                    done = (b - 1, 1) if unit == 1 else (b, 0)
                    for slot in range(QUAD):
                        if not last:
                            maxima(dve, b + 1, 1 - p, score_tiles(unit, slot))
                        if unit % 2 and not (first and unit == 1):
                            if slot == 0:
                                quad_sums(dve, *done)
                            if slot == 3:
                                quad_scale(dve, *done)
                        if unit == SCORE_UNITS and slot == 1 and not last:
                            negate(dve, b + 1, 1 - p)

            @block.vector
            def _(dve):
                for tile in (*q_stack, *k_stack):
                    nc.vector.memset(tile[:].bitcast(F32), 1.0).then_inc(blank, 1)
                for tile in wo:
                    nc.vector.memset(tile[:], 0.0).then_inc(blank, 1)
                dve.wait_ge(const_in, 16 * 11)
                dve.wait_ge(gated, 1)
                nc.vector.tensor_tensor(gate_bias[:], bias_o[:], keep["gates"][:, 0:1], ALU.mult).then_inc(blank, 1)
                maxima(dve, 0, 0, [(t // KT, t % KT, t) for t in range(TILES)])
                negate(dve, 0, 0)
                vector_step(dve, 0, 0, True, False)
                vector_step(dve, 1, 1, False, False)
                with dve.Fori(1, B // 2 - 1) as i:
                    for p in two:
                        vector_step(dve, i * 2 + p, p, False, False)
                vector_step(dve, B - 2, 0, False, False)
                vector_step(dve, B - 1, 1, False, True)
                quad_sums(dve, B - 1, 1)
                quad_scale(dve, B - 1, 1)

            def set_v(pool, b, p, first):
                pool.wait_ge(vx_in[p], (b // 2 if isinstance(b, int) else (b - p) // 2) * 32 + 32)
                if not first:
                    pool.wait_ge(pv_done, b * UNITS - UNITS)
                pool.sem_inc(pool_passed, 1)
                nc.gpsimd.tensor_copy(v_ones[p][:, :, :, 0:KC], v_in[p][:]).then_inc(v_set, 1)

            def residual(pool, b, p, first):
                pool.wait_ge(attn_ok, b + 1)
                if not first:
                    pool.wait_ge(x_stored[p], (b // 2 if isinstance(b, int) else (b - p) // 2) * 16)
                nc.gpsimd.tensor_tensor(x_out[p][:], x_in[p][:], attn[:], ALU.add).then_inc(x_ok, 1)

            @block.gpsimd
            def _(pool):
                for p in two:
                    nc.gpsimd.memset(v_ones[p][:], 1.0).then_inc(keep["v_blank"], 1)
                pool.wait_ge(keep["v_blank"], 2)
                set_v(pool, 0, 0, True)
                set_v(pool, 1, 1, True)
                residual(pool, 0, 0, True)
                set_v(pool, 2, 0, False)
                residual(pool, 1, 1, True)
                set_v(pool, 3, 1, False)
                with pool.Fori(1, B // 2 - 1) as i:
                    for p in two:
                        residual(pool, i * 2 + p, p, False)
                        set_v(pool, i * 2 + p + 2, p, False)
                for p in two:
                    residual(pool, B - 2 + p, p, False)


def feed_forward(nc, d, keep):
    with ExitStack() as ctx:
        sb = lambda name, shape, dt: ctx.enter_context(nc.sbuf_tensor(name, shape, dt))
        ps = lambda name, shape, dt: ctx.enter_context(nc.psum_tensor(name, shape, dt))
        sem = lambda name: ctx.enter_context(nc.semaphore(name))
        two = range(2)
        groups = B // GROUP
        xg = [sb(f"xg{p}", [P, GROUP, T], F32) for p in two]
        xn = sb("xn_ffn", [P, GROUP, T], F32)
        stats = sb("stats_ffn", [P, GROUP, 6], F32)
        moments = sb("moments_ffn", [P, GROUP, 2], F32)
        rstd = sb("rstd_ffn", [P, 2, GROUP], F32)
        eps = sb("eps_ffn", [P, 2], F32)
        x_head = sb("x_head", [P, KT, T], F32R)
        x_rest = sb("x_rest", [P, KT, T], F32R)
        x_bf16 = sb("x_bf16", [P, KT, T], BF16)
        silu = [sb(f"silu{p}", [P, T], F32) for p in two]
        hidden = [sb(f"hidden{p}", [P, T], F32) for p in two]
        h_head = [sb(f"h_head{p}", [P, T], F32R) for p in two]
        h_rest = [sb(f"h_rest{p}", [P, T], F32R) for p in two]
        h_bf16 = [sb(f"h_bf16{p}", [P, T], BF16) for p in two]
        squares = sb("squares", [P, GROUP, T], F32)
        rms = sb("rms", [P, 3, GROUP], F32)
        y_out = [sb(f"y_out{p}", [P, GROUP, T], F32) for p in two]
        gu_ps = [ps(f"gu_ps{p}", [P, 2, T], F32) for p in two]
        y_ps = ps("y_ps", [P, GROUP, T], F32)

        xg_in = [sem(f"xg_in{p}") for p in two]
        consts = sem("consts3")
        stat = sem("stat3")
        dev = sem("dev3")
        inv = sem("inv3")
        normed = sem("normed3")
        turned = sem("turned3")
        heads = sem("heads3")
        rests = sem("rests3")
        gu_done = sem("gu_done")
        silu_ok = sem("silu_ok")
        hid_ok = sem("hid_ok")
        h_heads = sem("h_heads")
        h_rests = sem("h_rests")
        h_bf16s = sem("h_bf16s")
        down = sem("down")
        squared = sem("squared")
        rooted = sem("rooted")
        scaled = sem("scaled3")
        y_ok = sem("y_ok")
        stored = [sem(f"stored3{p}") for p in two]

        with nc.Block() as block:
            @block.sync
            def _(sp):
                def load(g, p):
                    sp.dma_start(xg[p][:], keep["x_dram"][bass.ds(g * GROUP, GROUP)].rearrange("j p t -> p j t")).then_inc(xg_in[p], 16)

                def store(g, p):
                    sp.wait_ge(y_ok, g * GROUP + GROUP)
                    sp.dma_start(d["out"][bass.ds(g * GROUP, GROUP)].rearrange("j p t -> p j t"), y_out[p][:]).then_inc(stored[p], 16)

                for p in two:
                    load(p, p)
                with sp.Fori(0, groups // 2 - 1) as i:
                    for p in two:
                        g = i * 2 + p
                        store(g, p)
                        load(g + 2, p)
                for p in two:
                    store(groups - 2 + p, p)
                for p in two:
                    sp.wait_ge(stored[p], 16 * (groups // 2))

            def normalise(dve, g, i, p):
                dve.wait_ge(xg_in[p], i * 16 + 16)
                for j in range(GROUP):
                    nc.vector.bn_stats(stats[:, j, :], xg[p][:, j, :]).then_inc(stat, 1)
                for j in range(GROUP):
                    dve.wait_ge(stat, g * 8 + j + 1)
                    nc.vector.bn_aggr(moments[:, j, :], stats[:, j, :]).then_inc(stat, 1)
                dve.wait_ge(dev, g + 1)
                nc.vector.reciprocal(rstd[:, 1, :], rstd[:, 0, :]).then_inc(inv, 1)
                dve.wait_ge(inv, g + 1)
                for j in range(GROUP):
                    nc.vector.tensor_scalar(xn[:, j, :], xg[p][:, j, :], moments[:, j, 0:1], rstd[:, 1, j:j + 1],
                                            ALU.subtract, ALU.mult).then_inc(normed, 1)

            def vector_group(dve, i, p, last):
                g = i * 2 + p
                for k in range(KT):
                    dve.wait_ge(heads, g * 8 + 2 * k + 2)
                    nc.vector.tensor_tensor(x_rest[:, k], gu_ps[k // 2][:, k % 2], x_head[:, k].bitcast(F32),
                                            ALU.subtract).then_inc(rests, 1)
                for t in range(IT):
                    at = g * IT + t
                    dve.wait_ge(silu_ok, at + 1)
                    if not (isinstance(g, int) and g == 0 and t < 2):
                        dve.wait_ge(h_bf16s, at - 1)
                    nc.vector.tensor_tensor(hidden[t % 2][:], gu_ps[t % 2][:, 1], silu[t % 2][:], ALU.mult).then_inc(hid_ok, 1)
                    dve.wait_ge(h_heads, at + 1)
                    nc.vector.tensor_tensor(h_rest[t % 2][:], hidden[t % 2][:], h_head[t % 2][:].bitcast(F32),
                                            ALU.subtract).then_inc(h_rests, 1)
                    if t == IT // 2 and not last:
                        normalise(dve, g + 1, i + p, 1 - p)
                dve.wait_ge(rooted, g + 1)
                nc.vector.reciprocal(rms[:, 2, :], rms[:, 1, :]).then_inc(scaled, 1)
                dve.wait_ge(scaled, g * 2 + 1)
                nc.vector.tensor_scalar(rms[:, 2, :], rms[:, 2, :], keep["gates"][:, 1:2], None, ALU.mult).then_inc(scaled, 1)
                dve.wait_ge(scaled, g * 2 + 2)
                if not (isinstance(i, int) and i == 0):
                    dve.wait_ge(stored[p], i * 16)
                for j in range(GROUP):
                    nc.vector.scalar_tensor_tensor(y_out[p][:, j, :], y_ps[:, j, :], rms[:, 2, j:j + 1], xg[p][:, j, :],
                                                   ALU.mult, ALU.add).then_inc(y_ok, 1)

            @block.vector
            def _(dve):
                nc.vector.memset(eps[:, 0:1], LN_EPS).then_inc(consts, 1)
                nc.vector.memset(eps[:, 1:2], RMS_EPS).then_inc(consts, 1)
                normalise(dve, 0, 0, 0)
                vector_group(dve, 0, 0, False)
                vector_group(dve, 0, 1, False)
                if groups > 4:
                    with dve.Fori(1, groups // 2 - 1) as i:
                        for p in two:
                            vector_group(dve, i, p, False)
                vector_group(dve, groups // 2 - 1, 0, False)
                vector_group(dve, groups // 2 - 1, 1, True)

            def deviations(act, g):
                act.wait_ge(stat, g * 8 + 8)
                nc.scalar.activation(rstd[:, 0, :], moments[:, :, 1], ACT.Sqrt, bias=eps[:, 0:1]).then_inc(dev, 1)

            def scalar_group(act, g, last):
                for k in range(KT):
                    act.wait_ge(turned, g * KT + k + 1)
                    nc.scalar.activation(x_head[:, k], gu_ps[k // 2][:, k % 2], ACT.Copy).then_inc(heads, 1)
                    nc.scalar.activation(x_bf16[:, k], gu_ps[k // 2][:, k % 2], ACT.Copy).then_inc(heads, 1)
                for t in range(IT):
                    at = g * IT + t
                    act.wait_ge(gu_done, at + 1)
                    nc.scalar.activation(silu[t % 2][:], gu_ps[t % 2][:, 0], ACT.Silu).then_inc(silu_ok, 1)
                    act.wait_ge(hid_ok, at + 1)
                    if not (isinstance(g, int) and g == 0 and t < 2):
                        act.wait_ge(down, at - 1)
                    nc.scalar.activation(h_head[t % 2][:], hidden[t % 2][:], ACT.Copy).then_inc(h_heads, 1)
                    nc.scalar.activation(h_bf16[t % 2][:], hidden[t % 2][:], ACT.Copy).then_inc(h_bf16s, 1)
                    if t == IT // 2 and not last:
                        deviations(act, g + 1)
                act.wait_ge(down, g * IT + IT)
                for j in range(GROUP):
                    nc.scalar.activation(squares[:, j], y_ps[:, j, :], ACT.Square, accum_out=rms[:, 0, j:j + 1]).then_inc(squared, 1)
                act.wait_ge(squared, g * GROUP + GROUP)
                nc.scalar.activation(rms[:, 1, :], rms[:, 0, :], ACT.Sqrt, bias=eps[:, 1:2], scale=1.0 / T).then_inc(rooted, 1)

            @block.scalar
            def _(act):
                act.wait_ge(consts, 2)
                deviations(act, 0)
                scalar_group(act, 0, False)
                with act.Fori(1, groups - 1) as g:
                    scalar_group(act, g, False)
                scalar_group(act, groups - 1, True)

            def gate_up(pe, g, t):
                at = g * IT + t
                if t == 0:
                    pe.wait_ge(heads, g * 8 + 8)
                    pe.wait_ge(rests, g * 4 + 4)
                elif t > 1:
                    pe.wait_ge(hid_ok, at - 1)
                for half, col in ((0, t * P), (1, INNER + t * P)):
                    for k in range(KT):
                        head = keep["gu_head"][:, k, col:col + P]
                        nc.tensor.matmul(gu_ps[t % 2][:, half], head, x_head[:, k], start=(k == 0), stop=False)
                        nc.tensor.matmul(gu_ps[t % 2][:, half], head, x_rest[:, k], start=False, stop=False)
                    for k in range(KT):
                        last = nc.tensor.matmul(gu_ps[t % 2][:, half], keep["gu_rest"][:, k, col:col + P], x_bf16[:, k],
                                                start=False, stop=(k == KT - 1))
                last.then_inc(gu_done, 1)

            def project_down(pe, g, t, first):
                at = g * IT + t
                pe.wait_ge(h_heads, at + 1)
                pe.wait_ge(h_rests, at + 1)
                pe.wait_ge(h_bf16s, at + 1)
                if t == 0 and not first:
                    pe.wait_ge(y_ok, g * GROUP)
                for j in range(GROUP):
                    cols = slice(j * P, (j + 1) * P)
                    for n, (h, w) in enumerate(((h_head, "dn_head"), (h_rest, "dn_head"), (h_bf16, "dn_rest"))):
                        last = nc.tensor.matmul(y_ps[:, j, :], h[t % 2][:, cols], keep[w][:, t, :],
                                                start=(t == 0 and n == 0), stop=(t == IT - 1 and n == 2))
                last.then_inc(down, 1)

            def tensor_group(pe, g, first):
                pe.wait_ge(normed, g * GROUP + GROUP)
                if not first:
                    pe.wait_ge(hid_ok, g * IT)
                for k in range(KT):
                    for j in range(GROUP):
                        last = nc.tensor.transpose(gu_ps[k // 2][:, k % 2, j * P:(j + 1) * P], xn[:, j, k * P:(k + 1) * P],
                                                   keep["ident"][:])
                    last.then_inc(turned, 1)
                for t in range(IT):
                    gate_up(pe, g, t)
                    if t:
                        project_down(pe, g, t - 1, first)
                project_down(pe, g, IT - 1, first)

            @block.tensor
            def _(pe):
                tensor_group(pe, 0, True)
                with pe.Fori(1, groups) as g:
                    tensor_group(pe, g, False)


def build(nc, d):
    with ExitStack() as ctx:
        sb = lambda name, shape, dt: ctx.enter_context(nc.sbuf_tensor(name, shape, dt))
        keep = {
            "ident": sb("ident", [P, P], F32),
            "gates": sb("gates", [P, 2], F32),
            "gu_head": sb("gu_head", [P, KT, 2 * INNER], F32R),
            "gu_rest": sb("gu_rest", [P, KT, 2 * INNER], BF16),
            "dn_head": sb("dn_head", [P, IT, T], F32R),
            "dn_rest": sb("dn_rest", [P, IT, T], BF16),
            "qk_dram": nc.dram_tensor("qk_scratch", [B, 2, 2, P, T], F32).ap(),
            "v_dram": nc.dram_tensor("v_scratch", [B, P, T], F32).ap(),
            "x_dram": nc.dram_tensor("x_scratch", [B, P, T], F32).ap(),
            "v_blank": ctx.enter_context(nc.semaphore("v_blank")),
        }
        unpack_weights(nc, d, keep)
        project(nc, d, keep)
        attend(nc, d, keep)
        feed_forward(nc, d, keep)


def kernel(**inputs):
    import concourse.bacc as bacc
    from concourse.bass_utils import run_bass_kernel_spmd

    a = {k: np.ascontiguousarray(v) for k, v in inputs.items()}
    theta = (1.0 / np.float32(10000.0) ** (np.arange(0, ROT, 2, dtype=np.float32) / np.float32(ROT))).astype(np.float32)
    angle = np.arange(T, dtype=np.float32)[None, :] * np.concatenate([theta, theta])[:, None]
    turn = np.concatenate([-np.ones(ROT // 2, np.float32), np.ones(ROT // 2, np.float32)])[:, None]
    cos = np.concatenate([np.cos(angle), np.ones((KC - ROT, T), np.float32)])
    sin = np.concatenate([np.sin(angle) * turn, np.zeros((KC - ROT, T), np.float32)])
    arrays = {
        "x": a["x"], "ctx": a["ctx_2048"], "g_xattn": a["g_xattn"], "g_ffn": a["g_ffn"],
        "wqT": np.ascontiguousarray(a["L0_xattn_Wq"].T), "wkT": np.ascontiguousarray(a["L0_xattn_Wk"].T),
        "wvT": np.ascontiguousarray(a["L0_xattn_Wv"].T), "woT": np.ascontiguousarray(a["L0_xattn_Wo"].T),
        "bq": a["L0_xattn_bq"], "bk": a["L0_xattn_bk"], "bv": a["L0_xattn_bv"], "bo": a["L0_xattn_bo"],
        "gate_up_packed": a["L0_ffn_gate_up_packed"].view(np.uint32), "gate_up_scales": a["L0_ffn_gate_up_scales"],
        "down_packed": a["L0_ffn_down_packed"].view(np.uint32), "down_scales": a["L0_ffn_down_scales"],
        "cos": np.tile(cos, (HEADS, 1)).astype(np.float32), "sin": np.tile(sin, (HEADS, 1)).astype(np.float32),
        "ident": np.eye(P, dtype=np.float32),
    }
    nc = bacc.Bacc("TRN2", target_bir_lowering=False, num_devices=1)
    d = {name: nc.dram_tensor(name + "_dram", v.shape, mybir.dt.from_np(v.dtype), kind="ExternalInput").ap()
         for name, v in arrays.items()}
    d["out"] = nc.dram_tensor("out_dram", (B, P, T), F32, kind="ExternalOutput").ap()
    build(nc, d)
    r = run_bass_kernel_spmd(nc, [{name + "_dram": v for name, v in arrays.items()}], core_ids=[0])
    return r.results[0]["out_dram"]
```

```python
from contextlib import ExitStack

import numpy as np

import concourse.bass as bass
from concourse import mybir

ALU = mybir.AluOpType
ACT = mybir.ActivationFunctionType
AXIS_X = mybir.AxisListType.X
F32 = mybir.dt.float32
F32R = mybir.dt.float32r
BF16 = mybir.dt.bfloat16
F16 = mybir.dt.float16
FP8E3 = mybir.dt.float8e3
U32 = mybir.dt.uint32

P = 128
B = 16
T = 512
HEADS = 8
KC = P // HEADS
ROT = KC // 2
KT = T // P
INNER = 1408
IT = INNER // P
GU = 2 * INNER // P
LN_EPS = 1e-5
RMS_EPS = 1e-6
SCORE_SCALE = KC ** -0.5

STACK = 64
PARTS = 3
MAX_ROW = P - 1
QUAD = 4
GROUP = 4


def unpack_weights(nc, d, keep):
    with ExitStack() as ctx:
        sb = lambda name, shape, dt: ctx.enter_context(nc.sbuf_tensor(name, shape, dt))
        ps = lambda name, shape, dt: ctx.enter_context(nc.psum_tensor(name, shape, dt))
        sem = lambda name: ctx.enter_context(nc.semaphore(name))
        gu_words, dn_words = GU * T // 8, KT * INNER // 8
        words = gu_words + dn_words
        packed = sb("packed", [P, words], U32)
        part_a = sb("part_a", [P, words], U32)
        part_b = sb("part_b", [P, words], U32)
        sign = sb("sign", [P, words], U32)
        gu_vals = sb("gu_vals", [P, GU, 2, T // 2], BF16)
        dn_vals = sb("dn_vals", [P, KT, 2, INNER // 2], BF16)
        gu_sc16 = sb("gu_sc16", [KT * GU, P], F16)
        dn_sc16 = sb("dn_sc16", [IT * KT, P], F16)
        gu_sc32 = sb("gu_sc32", [KT * GU, P], F32)
        dn_sc32 = sb("dn_sc32", [IT * KT, P], F32)
        gu_sc = sb("gu_sc", [P, KT, GU], F32)
        dn_sc = sb("dn_sc", [P, IT, KT], F32)
        wtile = [sb(f"wtile{p}", [P, T], F32) for p in range(2)]
        wt_ps = [ps(f"wt_ps{p}", [P, KT, P], F32) for p in range(2)]
        sc_ps = ps("sc_ps", [P, KT * GU + IT * KT], F32)

        packed_in = sem("packed_in")
        scales_in = sem("scales_in")
        ident_in = sem("ident_in")
        bits = sem("bits")
        scales_f32 = sem("scales_f32")
        scales_t = sem("scales_t")
        scales_ok = sem("scales_ok")
        vals_ok = sem("vals_ok")
        scaled = sem("scaled")
        turned = sem("turned")
        heads = sem("heads")
        rests = sem("rests")
        chunks = [(t, g0, min(KT, IT - g0)) for t in range(KT) for g0 in range(0, IT, KT)]

        with nc.Block() as block:
            @block.sync
            def _(sp):
                sp.dma_start(packed[:, 0:gu_words].rearrange("p (t w) -> p t w", t=GU),
                             d["gate_up_packed"].rearrange("(t p) w -> p t w", p=P)).then_inc(packed_in, 16)
                sp.dma_start(packed[:, gu_words:words].rearrange("p (t w) -> p t w", t=KT),
                             d["down_packed"].rearrange("(t p) w -> p t w", p=P)).then_inc(packed_in, 16)
                sp.dma_start(gu_sc16[:], d["gate_up_scales"].rearrange("g (t o) -> (g t) o", o=P)).then_inc(scales_in, 16)
                sp.dma_start(dn_sc16[:], d["down_scales"].rearrange("g (t o) -> (g t) o", o=P)).then_inc(scales_in, 16)
                sp.dma_start(keep["ident"][:], d["ident"]).then_inc(ident_in, 16)

            @block.vector
            def _(dve):
                dve.wait_ge(packed_in, 32)
                nc.vector.tensor_scalar(part_a[:], packed[:], 0x07070707, 3, ALU.bitwise_and,
                                        ALU.logical_shift_left).then_inc(bits, 1)
                nc.vector.tensor_scalar(sign[:], packed[:], 0x08080808, 4, ALU.bitwise_and,
                                        ALU.logical_shift_left).then_inc(bits, 1)
                nc.vector.tensor_scalar(part_b[:], packed[:], 0x70707070, 1, ALU.bitwise_and,
                                        ALU.logical_shift_right).then_inc(bits, 1)
                dve.wait_ge(bits, 3)
                nc.vector.tensor_tensor(part_a[:], part_a[:], sign[:], ALU.bitwise_or).then_inc(bits, 1)
                nc.vector.tensor_scalar(packed[:], packed[:], 0x80808080, None, ALU.bitwise_and).then_inc(bits, 1)
                dve.wait_ge(bits, 5)
                nc.vector.tensor_tensor(part_b[:], part_b[:], packed[:], ALU.bitwise_or).then_inc(bits, 1)

                dve.wait_ge(scales_ok, 2)

                def scale_tile(buf, vals, scales, groups):
                    for odd in range(2):
                        out = buf[:, 0:groups * P].rearrange("p (g c two) -> p g c two", g=groups, two=2)[:, :, :, odd]
                        last = nc.vector.tensor_tensor(
                            out, vals[odd].rearrange("p (g c) -> p g c", g=groups),
                            scales.unsqueeze(2).to_broadcast([P, groups, P // 2]), ALU.mult)
                    last.then_inc(scaled, 1)

                def rest_tile(rest, head, tile_ps):
                    nc.vector.tensor_tensor(rest, tile_ps, head.bitcast(F32), ALU.subtract).then_inc(rests, 1)

                dve.wait_ge(vals_ok, 4)
                with dve.Fori(0, GU // 2) as i:
                    for p in range(2):
                        t = i * 2 + p
                        scale_tile(wtile[p], [gu_vals[:, bass.ds(t, 1), o, :].rearrange("p a c -> p (a c)") for o in range(2)],
                                   gu_sc[:, :, bass.ds(t, 1)].rearrange("p g a -> p (g a)"), KT)
                        dve.wait_ge(heads, t + 1)
                        rest_tile(keep["gu_rest"][:, :, bass.ds(t * P, P)], keep["gu_head"][:, :, bass.ds(t * P, P)],
                                  wt_ps[p][:])
                for n, (t, g0, groups) in enumerate(chunks):
                    p, at = n % 2, GU + n
                    scale_tile(wtile[p], [dn_vals[:, t, o, g0 * 64:(g0 + groups) * 64] for o in range(2)],
                               dn_sc[:, g0:g0 + groups, t], groups)
                    dve.wait_ge(heads, at + 1)
                    rest_tile(keep["dn_rest"][:, g0:g0 + groups, t * P:(t + 1) * P],
                              keep["dn_head"][:, g0:g0 + groups, t * P:(t + 1) * P], wt_ps[p][:, 0:groups, :])

            @block.scalar
            def _(act):
                act.wait_ge(scales_in, 32)
                nc.scalar.activation(gu_sc32[:], gu_sc16[:], ACT.Copy, scale=4.0).then_inc(scales_f32, 1)
                nc.scalar.activation(dn_sc32[:], dn_sc16[:], ACT.Copy, scale=4.0).then_inc(scales_f32, 1)
                act.wait_ge(scales_t, 2)
                nc.scalar.activation(gu_sc[:].rearrange("p g t -> p (g t)"), sc_ps[:, 0:KT * GU], ACT.Copy).then_inc(scales_ok, 1)
                nc.scalar.activation(dn_sc[:].rearrange("p g t -> p (g t)"), sc_ps[:, KT * GU:], ACT.Copy).then_inc(scales_ok, 1)
                for odd, part, need in ((0, part_a, 4), (1, part_b, 6)):
                    act.wait_ge(bits, need)
                    by = part[:].bitcast(FP8E3)
                    nc.scalar.activation(gu_vals[:, :, odd, :], by[:, 0:4 * gu_words].rearrange("p (t c) -> p t c", t=GU),
                                         ACT.Copy).then_inc(vals_ok, 1)
                    nc.scalar.activation(dn_vals[:, :, odd, :], by[:, 4 * gu_words:].rearrange("p (t c) -> p t c", t=KT),
                                         ACT.Copy).then_inc(vals_ok, 1)
                with act.Fori(0, GU // 2) as i:
                    for p in range(2):
                        t = i * 2 + p
                        act.wait_ge(turned, t + 1)
                        nc.scalar.activation(keep["gu_head"][:, :, bass.ds(t * P, P)], wt_ps[p][:], ACT.Copy).then_inc(heads, 1)
                for n, (t, g0, groups) in enumerate(chunks):
                    act.wait_ge(turned, GU + n + 1)
                    nc.scalar.activation(keep["dn_head"][:, g0:g0 + groups, t * P:(t + 1) * P],
                                         wt_ps[n % 2][:, 0:groups, :], ACT.Copy).then_inc(heads, 1)

            @block.tensor
            def _(pe):
                pe.wait_ge(ident_in, 16)
                pe.wait_ge(scales_f32, 2)
                nc.tensor.transpose(sc_ps[:, 0:KT * GU], gu_sc32[:], keep["ident"][0:KT * GU, 0:KT * GU]).then_inc(scales_t, 1)
                nc.tensor.transpose(sc_ps[:, KT * GU:], dn_sc32[:], keep["ident"][0:IT * KT, 0:IT * KT]).then_inc(scales_t, 1)

                def turn(p, groups):
                    for k in range(groups):
                        last = nc.tensor.transpose(wt_ps[p][:, k, :], wtile[p][:, k * P:(k + 1) * P], keep["ident"][:])
                    last.then_inc(turned, 1)

                with pe.Fori(0, GU // 2) as i:
                    for p in range(2):
                        pe.wait_ge(scaled, i * 2 + p + 1)
                        turn(p, KT)
                for n, (t, g0, groups) in enumerate(chunks):
                    pe.wait_ge(scaled, GU + n + 1)
                    turn(n % 2, groups)


STORES = 16 * 5


def project(nc, d, keep):
    with ExitStack() as ctx:
        sb = lambda name, shape, dt: ctx.enter_context(nc.sbuf_tensor(name, shape, dt))
        ps = lambda name, shape, dt: ctx.enter_context(nc.psum_tensor(name, shape, dt))
        sem = lambda name: ctx.enter_context(nc.semaphore(name))
        wq, wk, wv = (sb(n, [P, P], F32) for n in ("wq", "wk", "wv"))
        bias_q, bias_qs, bias_k = (sb(n, [P, 1], F32) for n in ("bias_q", "bias_qs", "bias_k"))
        bias_v = sb("bias_v", [P, P], F32)
        eps = sb("ln_eps", [P, 1], F32)
        cos, sin = sb("cos", [P, T], F32), sb("sin", [P, T], F32)
        two = range(2)
        xt = [sb(f"xt{p}", [P, T], F32) for p in two]
        ct = [sb(f"ct{p}", [P, T], F32) for p in two]
        xn = [sb(f"xn{p}", [P, T], F32) for p in two]
        stats = [sb(f"stats{p}", [P, 6], F32) for p in two]
        moments = [sb(f"moments{p}", [P, 2], F32) for p in two]
        rstd = [sb(f"rstd{p}", [P, 2], F32) for p in two]
        proj = [sb(f"proj{p}", [P, 2, T], F32) for p in two]
        swap = [sb(f"swap{p}", [P, 2, T], F32) for p in two]
        by_cos = [sb(f"by_cos{p}", [P, 2, T], F32) for p in two]
        split = [sb(f"split{p}", [P, 2, 2, T], F32R) for p in two]
        vt = [sb(f"vt{p}", [P, KT, HEADS, 2 * KC], F32) for p in two]
        q_ps = [ps(f"q_ps{p}", [P, T], F32) for p in two]
        k_ps = [ps(f"k_ps{p}", [P, T], F32) for p in two]
        v_ps = [ps(f"v_ps{p}", [P, T], F32) for p in two]

        const_in = sem("const_in")
        loaded = [sem(f"loaded{p}") for p in two]
        stored = [sem(f"stored{p}") for p in two]
        consts = sem("consts")
        stat = sem("stat")
        dev = sem("dev")
        inv = sem("inv")
        normed = sem("normed")
        projected = sem("projected")
        biased = sem("biased")
        swapped = sem("swapped")
        cosine = sem("cosine")
        rotated = sem("rotated")
        heads = sem("heads1")
        rests = sem("rests1")
        passed = sem("passed1")
        v_ready = sem("v_ready")
        partner = [(i // KC) * KC + ((i % KC + ROT // 2) % ROT if i % KC < ROT else i % KC) for i in range(32)]

        with nc.Block() as block:
            @block.sync
            def _(sp):
                for out, name in ((wq, "wqT"), (wk, "wkT"), (wv, "wvT"), (cos, "cos"), (sin, "sin")):
                    sp.dma_start(out[:], d[name]).then_inc(const_in, 16)
                sp.dma_start(bias_q[:], d["bq"].rearrange("(p a) -> p a", a=1)).then_inc(const_in, 16)
                sp.dma_start(bias_k[:], d["bk"].rearrange("(p a) -> p a", a=1)).then_inc(const_in, 16)
                sp.dma_start(bias_v[:], d["bv"].rearrange("(a n) -> a n", a=1).to_broadcast([P, P])).then_inc(const_in, 16)

                def load(b, p):
                    sp.dma_start(xt[p][:], d["x"][bass.ds(b, 1)].rearrange("a p t -> (a p) t")).then_inc(loaded[p], 16)
                    sp.dma_start(ct[p][:], d["ctx"][bass.ds(b, 1)].rearrange("a p t -> (a p) t")).then_inc(loaded[p], 16)

                def store(b, p):
                    for w in two:
                        for s in two:
                            sp.dma_start(keep["qk_dram"][bass.ds(b, 1), w, :, s].rearrange("a h c t -> (a h) c t"),
                                         split[p][:, w, s].bitcast(F32)).then_inc(stored[p], 16)
                    sp.dma_start(keep["v_dram"][bass.ds(b, 1)].rearrange("a p t -> (a p) t"),
                                 vt[p][:].rearrange("p k h c -> p (k h c)")).then_inc(stored[p], 16)

                for p in two:
                    load(p, p)
                with sp.Fori(0, B // 2 - 1) as i:
                    for p in two:
                        b = i * 2 + p
                        sp.wait_ge(projected, b + 1)
                        load(b + 2, p)
                        sp.wait_ge(rests, 2 * b + 2)
                        sp.wait_ge(v_ready, b + 1)
                        store(b, p)
                for p in two:
                    b = B - 2 + p
                    sp.wait_ge(rests, 2 * b + 2)
                    sp.wait_ge(v_ready, b + 1)
                    store(b, p)
                for p in two:
                    sp.wait_ge(stored[p], STORES * (B // 2))

            def vector_step(dve, i, p, first):
                b = i * 2 + p
                dve.wait_ge(loaded[p], i * 32 + 32)
                nc.vector.bn_stats(stats[p][:], xt[p][:]).then_inc(stat, 1)
                dve.wait_ge(stat, b * 2 + 1)
                dve.sem_inc(passed, 1)
                nc.vector.bn_aggr(moments[p][:], stats[p][:]).then_inc(stat, 1)
                dve.wait_ge(dev, b + 1)
                nc.vector.reciprocal(rstd[p][:, 1:2], rstd[p][:, 0:1]).then_inc(inv, 1)
                dve.wait_ge(inv, b + 1)
                nc.vector.tensor_scalar(xn[p][:], xt[p][:], moments[p][:, 0:1], rstd[p][:, 1:2], ALU.subtract,
                                        ALU.mult).then_inc(normed, 1)

            def vector_rotate(dve, i, p, first):
                b = i * 2 + p
                for w in two:
                    dve.wait_ge(biased, b * 2 + w + 1)
                    if not first:
                        dve.wait_ge(rests, b * 2 - 4 + w + 1)
                    dve.sem_inc(passed, 1)
                    nc.vector.stream_shuffle(swap[p][:, w], proj[p][:, w], partner).then_inc(swapped, 1)
                    dve.wait_ge(swapped, b * 4 + 2 * w + 1)
                    nc.vector.tensor_tensor(swap[p][:, w], swap[p][:, w], sin[:], ALU.mult).then_inc(swapped, 1)
                dve.wait_ge(projected, b + 1)
                if not first:
                    dve.wait_ge(stored[p], i * STORES)
                nc.vector.tensor_tensor(vt[p][:, :, :, 0:KC],
                                        v_ps[p][:].rearrange("p (k h c) -> p k h c", k=KT, c=KC),
                                        bias_v[:].rearrange("p (h c) -> p h c", c=KC).unsqueeze(1).to_broadcast([P, KT, HEADS, KC]),
                                        ALU.add).then_inc(v_ready, 1)
                for w in two:
                    dve.wait_ge(swapped, b * 4 + 2 * w + 2)
                    dve.wait_ge(cosine, b * 2 + w + 1)
                    nc.vector.tensor_tensor(swap[p][:, w], swap[p][:, w], by_cos[p][:, w], ALU.add).then_inc(rotated, 1)

            @block.vector
            def _(dve):
                dve.wait_ge(const_in, 16 * 8)
                nc.vector.tensor_scalar(bias_qs[:], bias_q[:], SCORE_SCALE, None, ALU.mult).then_inc(consts, 1)
                nc.vector.memset(eps[:], LN_EPS).then_inc(consts, 1)
                for p in two:
                    nc.vector.memset(vt[p][:], 1.0).then_inc(consts, 1)
                dve.wait_ge(consts, 4)
                vector_step(dve, 0, 0, True)
                vector_step(dve, 0, 1, True)
                vector_rotate(dve, 0, 0, True)
                vector_step(dve, 1, 0, False)
                vector_rotate(dve, 0, 1, True)
                vector_step(dve, 1, 1, False)
                with dve.Fori(1, B // 2 - 1) as i:
                    for p in two:
                        vector_rotate(dve, i, p, False)
                        vector_step(dve, i + 1, p, False)
                for p in two:
                    vector_rotate(dve, B // 2 - 1, p, False)

            def scalar_dev(act, i, p):
                b = i * 2 + p
                act.wait_ge(stat, b * 2 + 2)
                nc.scalar.activation(rstd[p][:, 0:1], moments[p][:, 1:2], ACT.Sqrt, bias=eps[:]).then_inc(dev, 1)

            def scalar_split(act, i, p, first):
                b = i * 2 + p
                act.wait_ge(projected, b + 1)
                if not first:
                    act.wait_ge(cosine, b * 2 - 2)
                nc.scalar.activation(proj[p][:, 0], q_ps[p][:], ACT.Identity, bias=bias_qs[:], scale=SCORE_SCALE).then_inc(biased, 1)
                nc.scalar.activation(proj[p][:, 1], k_ps[p][:], ACT.Identity, bias=bias_k[:]).then_inc(biased, 1)
                for w in two:
                    act.wait_ge(rotated, b * 2 + w + 1)
                    if not first:
                        act.wait_ge(stored[p], i * STORES)
                    nc.scalar.activation(split[p][:, w, 0], swap[p][:, w], ACT.Copy).then_inc(heads, 1)

            @block.scalar
            def _(act):
                act.wait_ge(consts, 2)
                scalar_dev(act, 0, 0)
                scalar_dev(act, 0, 1)
                scalar_split(act, 0, 0, True)
                scalar_dev(act, 1, 0)
                scalar_split(act, 0, 1, True)
                scalar_dev(act, 1, 1)
                with act.Fori(1, B // 2 - 1) as i:
                    for p in two:
                        scalar_split(act, i, p, False)
                        scalar_dev(act, i + 1, p)
                for p in two:
                    scalar_split(act, B // 2 - 1, p, False)

            def pool_step(pool, i, p, first):
                b = i * 2 + p
                for w in two:
                    pool.wait_ge(biased, b * 2 + w + 1)
                    nc.gpsimd.tensor_tensor(by_cos[p][:, w], proj[p][:, w], cos[:], ALU.mult).then_inc(cosine, 1)
                for w in two:
                    pool.wait_ge(heads, b * 2 + w + 1)
                    if not first:
                        pool.wait_ge(stored[p], i * STORES)
                    nc.gpsimd.tensor_tensor(split[p][:, w, 1], swap[p][:, w], split[p][:, w, 0].bitcast(F32),
                                            ALU.subtract).then_inc(rests, 1)

            @block.gpsimd
            def _(pool):
                pool.wait_ge(const_in, 16 * 8)
                for p in two:
                    pool_step(pool, 0, p, True)
                with pool.Fori(1, B // 2) as i:
                    for p in two:
                        pool_step(pool, i, p, False)

            def tensor_step(pe, i, p, first):
                b = i * 2 + p
                pe.wait_ge(normed, b + 1)
                pe.wait_ge(loaded[p], i * 32 + 32)
                if not first:
                    pe.wait_ge(biased, b * 2 - 2)
                    pe.wait_ge(v_ready, b - 1)
                nc.tensor.matmul(q_ps[p][:], wq[:], xn[p][:], start=True, stop=True)
                nc.tensor.matmul(k_ps[p][:], wk[:], ct[p][:], start=True, stop=True)
                for k in range(KT):
                    last = nc.tensor.matmul(v_ps[p][:, k * P:(k + 1) * P], ct[p][:, k * P:(k + 1) * P], wv[:],
                                            start=True, stop=True)
                last.then_inc(projected, 1)

            @block.tensor
            def _(pe):
                pe.wait_ge(const_in, 16 * 8)
                for p in two:
                    tensor_step(pe, 0, p, True)
                with pe.Fori(1, B // 2) as i:
                    for p in two:
                        tensor_step(pe, i, p, False)


UNITS = 4
TILES = HEADS * KT
PER_SLOT = TILES // (UNITS * QUAD)
HALF_LOADS = 8


def score_tiles(unit, slot):
    ahead, n = (2, 0) if unit == UNITS - 1 else (1, unit + 1)
    first = (n * QUAD + slot) * PER_SLOT
    return ahead, list(range(first, first + PER_SLOT))


def attend(nc, d, keep):
    with ExitStack() as ctx:
        sb = lambda name, shape, dt: ctx.enter_context(nc.sbuf_tensor(name, shape, dt))
        ps = lambda name, shape, dt: ctx.enter_context(nc.psum_tensor(name, shape, dt))
        sem = lambda name: ctx.enter_context(nc.semaphore(name))
        two = range(2)
        q_stack = [sb(f"q_stack{p}", [P, HEADS, T], F32R) for p in two]
        k_stack = [sb(f"k_stack{p}", [P, HEADS // 2, T], F32R) for p in two]
        v_ones = [sb(f"v_ones{p}", [P, KT, HEADS, 2 * KC], F32) for p in two]
        x_res = [sb(f"x_res{p}", [P, T], F32) for p in two]
        probs = [sb(f"probs{p}", [P, QUAD, 2, T], F32) for p in two]
        row_max = [sb(f"row_max{p}", [P, HEADS, KT], F32) for p in two]
        neg_max = [sb(f"neg_max{p}", [HEADS * KT, P], F32R) for p in two]
        sums_of = sb("pv_sb", [P, T], F32)
        scale_of = sb("scale_of", [P, T], F32)
        heads_out = [sb(f"heads_out{q}", [P, T], F32) for q in two]
        attn = sb("attn", [P, T], F32)
        wo = [sb(f"wo{q}", [P, P], F32) for q in two]
        bias_o, gate_bias = sb("bias_o", [P, 1], F32), sb("gate_bias", [P, 1], F32)
        gate_in = sb("gate_in", [P, 2], F32)

        st_ps = [ps(f"st_ps{p}", [P, 2, T], F32) for p in two]
        s_ps = [ps(f"s_ps{p}", [P, T], F32) for p in two]
        pv_ps = ps("pv_ps", [P, T], F32)
        misc_ps = ps("misc_ps", [P, T], F32)

        const_in = sem("const2_in")
        blank = sem("blank")
        gated = sem("gated")
        half_in = [[sem(f"half_in{p}{h}") for h in two] for p in two]
        v_in = [sem(f"v_in{p}") for p in two]
        x_in = [sem(f"x_in{p}") for p in two]
        scored = sem("scored")
        maxed = sem("maxed")
        max_turned = sem("max_turned")
        max_neg = sem("max_neg")
        max_in = [sem(f"max_in{p}") for p in two]
        st_done = sem("st_done")
        expd = sem("expd")
        pv_done = sem("pv_done")
        pv_out = sem("pv_out")
        passed = sem("passed2")
        sums_up = sem("sums_up")
        logs = sem("logs")
        inverses = sem("inverses")
        quad_done = sem("quad_done")
        mixed = sem("mixed")
        attn_ok = sem("attn_ok")
        x_ok = sem("x_ok")
        x_stored = [sem(f"x_stored{p}") for p in two]
        spread = [KC + i % KC for i in range(32)]

        with nc.Block() as block:
            def load_half(sp, b, p, h):
                slots = slice(2 * h, 2 * h + 2)
                for stack, which, parts in ((q_stack, 0, ((0, 0, 2), (2, 0, 1))), (k_stack, 1, ((0, 0, 1), (1, 0, 2)))):
                    src = keep["qk_dram"][bass.ds(b, 1), which].rearrange("a (j two) s c t -> two (a s c) j t", two=2)
                    for odd in two:
                        for row, part, n in parts:
                            at = STACK * odd + KC * row
                            rows = stack[p][at:at + n * KC, :, :].bitcast(F32)
                            if which == 0:
                                rows = rows.rearrange("c (j two) t -> c j two t", two=2)[:, :, odd, :]
                            sp.dma_start(rows[:, slots, :], src[odd, part * KC:(part + n) * KC, slots, :]).then_inc(half_in[p][h], 16)

            def load_v(sp, b, p):
                sp.dma_start(v_ones[p][:].rearrange("p k h c -> p (k h c)"),
                             keep["v_dram"][bass.ds(b, 1)].rearrange("a p t -> (a p) t")).then_inc(v_in[p], 16)

            def load_max(sp, b, p):
                sp.wait_ge(max_neg, b + 1)
                sp.dma_start(q_stack[p][MAX_ROW:MAX_ROW + 1, :, :].bitcast(F32).rearrange("a h t -> a (h t)"),
                             neg_max[p][:].bitcast(F32)).then_inc(max_in[p], 16)

            def sync_step(sp, b, p, first, ahead):
                if not first:
                    sp.wait_ge(st_done, b * 16)
                    load_half(sp, b + 1, 1 - p, 1)
                    sp.wait_ge(pv_done, b * UNITS)
                    load_v(sp, b + 1, 1 - p)
                if ahead:
                    sp.wait_ge(st_done, b * 16 + 8)
                    load_half(sp, b + 2, p, 0)
                load_max(sp, b + 1, 1 - p)

            @block.sync
            def _(sp):
                sp.wait_ge(blank, 6)
                for q in two:
                    for j in range(QUAD):
                        rows = slice((q * QUAD + j) * KC, (q * QUAD + j + 1) * KC)
                        sp.dma_start(wo[q][2 * KC * j:2 * KC * j + KC, :], d["woT"][rows, :]).then_inc(const_in, 16)
                sp.dma_start(bias_o[:], d["bo"].rearrange("(p a) -> p a", a=1)).then_inc(const_in, 16)
                sp.dma_start(gate_in[:, 0:1], d["g_xattn"].rearrange("(a n) -> a n", a=1).to_broadcast([P, 1])).then_inc(const_in, 16)
                sp.dma_start(gate_in[:, 1:2], d["g_ffn"].rearrange("(a n) -> a n", a=1).to_broadcast([P, 1])).then_inc(const_in, 16)
                for b in two:
                    load_half(sp, b, b, 0)
                    load_half(sp, b, b, 1)
                    load_v(sp, b, b)
                load_max(sp, 0, 0)
                sync_step(sp, 0, 0, True, True)
                sync_step(sp, 1, 1, False, True)
                with sp.Fori(1, B // 2 - 1) as i:
                    for p in two:
                        sync_step(sp, i * 2 + p, p, False, True)
                sync_step(sp, B - 2, 0, False, False)

            def score(pe, b, p, tiles):
                rows = slice(0, MAX_ROW)
                for n in tiles:
                    head, qt = n // KT, n % KT
                    at = b * TILES + n
                    if n == 0:
                        pe.wait_ge(half_in[p][0], (b // 2 if isinstance(b, int) else (b - p) // 2) * 16 * HALF_LOADS + 16 * HALF_LOADS)
                    if n == TILES // 2:
                        pe.wait_ge(half_in[p][1], (b // 2 if isinstance(b, int) else (b - p) // 2) * 16 * HALF_LOADS + 16 * HALF_LOADS)
                    if not (isinstance(b, int) and at < 2):
                        pe.wait_ge(maxed, at - 1)
                    nc.tensor.matmul(s_ps[n % 2][:], q_stack[p][rows, head, qt * P:(qt + 1) * P],
                                     k_stack[p][rows, head // 2, :], start=True, stop=True).then_inc(scored, 1)

            def turn_max(pe, b, p, first):
                pe.wait_ge(maxed, b * TILES + TILES)
                if not first:
                    pe.wait_ge(attn_ok, b - 1)
                nc.tensor.transpose(misc_ps[0:HEADS * KT, 0:P], row_max[p][:].rearrange("p h k -> p (h k)"),
                                    keep["ident"][:]).then_inc(max_turned, 1)

            def values(pe, b, p, half, part):
                quad = half // 2
                at = b * UNITS + half
                kt, cols = 2 * (half % 2) + part // 2, slice(T // 2 * (part % 2), T // 2 * (part % 2 + 1))
                if part == 0:
                    pe.wait_ge(expd, at * QUAD + QUAD)
                    if half == 0:
                        pe.wait_ge(v_in[p], (b // 2 if isinstance(b, int) else (b - p) // 2) * 16 + 16)
                    if half % 2 == 0 and not (isinstance(b, int) and b == 0 and quad == 0):
                        pe.wait_ge(pv_out, b * 2 + quad)
                for j in range(QUAD):
                    rows = slice(2 * KC * j, 2 * KC * (j + 1))
                    last = nc.tensor.matmul(pv_ps[rows, cols], v_ones[p][:, kt, quad * QUAD + j, :],
                                            probs[half % 2][:, j, part // 2, cols], start=(kt == 0 and part % 2 == 0),
                                            stop=(kt == KT - 1 and part % 2 == 1))
                if part == 3:
                    last.then_inc(pv_done, 1)

            def mix(pe, b, p):
                pe.wait_ge(quad_done, b * 2 + 2)
                pe.wait_ge(max_neg, B if isinstance(b, int) and b == B - 1 else b + 2)
                for q in two:
                    last = nc.tensor.matmul(misc_ps[:], wo[q][:], heads_out[q][:], start=(q == 0), stop=(q == 1))
                last.then_inc(mixed, 1)

            def tensor_step(pe, b, p, first, left):
                for unit in range(UNITS):
                    for slot in range(QUAD):
                        at = b * 16 + unit * QUAD + slot
                        ahead, tiles = score_tiles(unit, slot)
                        if ahead > left:
                            tiles = []
                        score(pe, b + ahead, (p + ahead) % 2, tiles[:1])
                        if unit == 0 and slot == 0:
                            pe.wait_ge(max_in[p], (b // 2 if isinstance(b, int) else (b - p) // 2) * 16 + 16)
                        if not (first and unit == 0 and slot < 2):
                            pe.wait_ge(expd, at - 1)
                        head = (unit // 2) * QUAD + slot
                        for k in range(2):
                            kt = 2 * (unit % 2) + k
                            mm = nc.tensor.matmul(st_ps[slot % 2][:, k, :], k_stack[p][:, head // 2, kt * P:(kt + 1) * P],
                                                  q_stack[p][:, head, :], start=True, stop=True)
                        mm.then_inc(st_done, 1)
                        if unit == UNITS - 1 and slot == 0 and left:
                            turn_max(pe, b + 1, 1 - p, first)
                        score(pe, b + ahead, (p + ahead) % 2, tiles[1:])
                        if unit:
                            values(pe, b, p, unit - 1, slot)
                        elif not first:
                            values(pe, b - 1, 1 - p, UNITS - 1, slot)
                        if unit == 2 and slot == 2 and not first:
                            mix(pe, b - 1, 1 - p)

            @block.tensor
            def _(pe):
                pe.wait_ge(const_in, 16 * 11)
                score(pe, 0, 0, range(TILES))
                turn_max(pe, 0, 0, True)
                score(pe, 1, 1, range(TILES // UNITS))
                tensor_step(pe, 0, 0, True, 2)
                tensor_step(pe, 1, 1, False, 2)
                with pe.Fori(1, B // 2 - 1) as i:
                    for p in two:
                        tensor_step(pe, i * 2 + p, p, False, 2)
                tensor_step(pe, B - 2, 0, False, 1)
                tensor_step(pe, B - 1, 1, False, 0)
                for part in range(QUAD):
                    values(pe, B - 1, 1, UNITS - 1, part)
                mix(pe, B - 1, 1)

            def quad_out(act, b, quad):
                act.wait_ge(pv_done, b * UNITS + 2 * quad + 2)
                if not (isinstance(b, int) and b == 0 and quad == 0):
                    act.wait_ge(quad_done, b * 2 + quad)
                nc.scalar.activation(sums_of[:], pv_ps[:], ACT.Copy).then_inc(pv_out, 1)

            def quad_inverse(act, b, quad):
                act.wait_ge(sums_up, b * 2 + quad + 1)
                nc.scalar.activation(scale_of[:], scale_of[:], ACT.Ln).then_inc(logs, 1)
                act.wait_ge(logs, b * 2 + quad + 1)
                nc.scalar.activation(scale_of[:], scale_of[:], ACT.Exp, scale=-1.0).then_inc(inverses, 1)

            def gate(act, b):
                act.wait_ge(mixed, b + 1)
                if not (isinstance(b, int) and b == 0):
                    act.wait_ge(x_ok, b)
                nc.scalar.activation(attn[:], misc_ps[:], ACT.Identity, bias=gate_bias[:], scale=keep["gates"][:, 0:1]).then_inc(attn_ok, 1)

            def scalar_step(act, b, p, first):
                for unit in range(UNITS):
                    done = (b - 1, 1) if unit == 1 else (b, 0)
                    for slot in range(QUAD):
                        if slot == 0 and unit % 2 and not (first and unit == 1):
                            quad_out(act, *done)
                        at = b * 16 + unit * QUAD + slot
                        act.wait_ge(st_done, at + 1)
                        if slot == 0 and not (first and unit < 2):
                            act.wait_ge(pv_done, b * UNITS + unit - 1)
                        nc.scalar.activation(probs[unit % 2][:, slot], st_ps[slot % 2][:], ACT.Exp).then_inc(expd, 1)
                        if slot == 2 and unit % 2 and not (first and unit == 1):
                            quad_inverse(act, *done)
                        if slot == 0 and unit == 3 and not first:
                            gate(act, b - 1)

            @block.scalar
            def _(act):
                act.wait_ge(const_in, 16 * 11)
                nc.scalar.activation(keep["gates"][:], gate_in[:], ACT.Tanh).then_inc(gated, 1)
                nc.scalar.preload_act_table_set("natural_log_exp_and_others")
                act.wait_ge(blank, 7)
                scalar_step(act, 0, 0, True)
                scalar_step(act, 1, 1, False)
                with act.Fori(1, B // 2) as i:
                    for p in two:
                        scalar_step(act, i * 2 + p, p, False)
                quad_out(act, B - 1, 1)
                quad_inverse(act, B - 1, 1)
                gate(act, B - 1)

            def maxima(dve, b, p, tiles):
                for n in tiles:
                    head, qt = n // KT, n % KT
                    dve.wait_ge(scored, b * TILES + n + 1)
                    if n == 0 and not (isinstance(b, int) and b < 2):
                        dve.wait_ge(max_turned, b - 1)
                    nc.vector.tensor_reduce(row_max[p][:, head, qt:qt + 1], s_ps[n % 2][:], AXIS_X,
                                            ALU.max).then_inc(maxed, 1)

            def negate(dve, b, p):
                dve.wait_ge(max_turned, b + 1)
                if not (isinstance(b, int) and b < 2):
                    dve.wait_ge(max_in[p], (b // 2 if isinstance(b, int) else (b - p) // 2) * 16)
                nc.vector.tensor_scalar(neg_max[p][:], misc_ps[0:HEADS * KT, 0:P], -1.0, None, ALU.mult).then_inc(max_neg, 1)

            def quad_sums(dve, b, quad):
                dve.wait_ge(pv_out, b * 2 + quad + 1)
                dve.sem_inc(passed, 1)
                nc.vector.stream_shuffle(scale_of[:], sums_of[:], spread).then_inc(sums_up, 1)

            def quad_scale(dve, b, quad):
                dve.wait_ge(inverses, b * 2 + quad + 1)
                if not (isinstance(b, int) and b == 0):
                    dve.wait_ge(mixed, b)
                nc.vector.tensor_tensor(heads_out[quad][:], sums_of[:], scale_of[:], ALU.mult).then_inc(quad_done, 1)

            def vector_step(dve, b, p, first, left):
                for unit in range(UNITS):
                    done = (b - 1, 1) if unit == 1 else (b, 0)
                    for slot in range(QUAD):
                        ahead, tiles = score_tiles(unit, slot)
                        if ahead <= left:
                            maxima(dve, b + ahead, (p + ahead) % 2, tiles)
                        if unit % 2 and not (first and unit == 1):
                            if slot == 0:
                                quad_sums(dve, *done)
                            if slot == 3:
                                quad_scale(dve, *done)
                        if unit == UNITS - 1 and slot == 0 and left:
                            negate(dve, b + 1, 1 - p)

            @block.vector
            def _(dve):
                for tile in q_stack:
                    nc.vector.memset(tile[:].bitcast(F32), 0.0).then_inc(blank, 1)
                for tile in k_stack:
                    nc.vector.memset(tile[:].bitcast(F32), 1.0).then_inc(blank, 1)
                for tile in wo:
                    nc.vector.memset(tile[:], 0.0).then_inc(blank, 1)
                dve.wait_ge(const_in, 16 * 11)
                dve.wait_ge(gated, 1)
                nc.vector.tensor_tensor(gate_bias[:], bias_o[:], keep["gates"][:, 0:1], ALU.mult).then_inc(blank, 1)
                maxima(dve, 0, 0, range(TILES))
                negate(dve, 0, 0)
                maxima(dve, 1, 1, range(TILES // UNITS))
                vector_step(dve, 0, 0, True, 2)
                vector_step(dve, 1, 1, False, 2)
                with dve.Fori(1, B // 2 - 1) as i:
                    for p in two:
                        vector_step(dve, i * 2 + p, p, False, 2)
                vector_step(dve, B - 2, 0, False, 1)
                vector_step(dve, B - 1, 1, False, 0)
                quad_sums(dve, B - 1, 1)
                quad_scale(dve, B - 1, 1)

            def load_x(pool, b, p):
                pool.dma_start(x_res[p][:], d["x"][bass.ds(b, 1)].rearrange("a p t -> (a p) t")).then_inc(x_in[p], 16)

            def residual(pool, b, p, i, load):
                pool.wait_ge(x_in[p], i * 16 + 16)
                pool.wait_ge(attn_ok, b + 1)
                nc.gpsimd.tensor_tensor(x_res[p][:], x_res[p][:], attn[:], ALU.add).then_inc(x_ok, 1)
                pool.wait_ge(x_ok, b + 1)
                pool.dma_start(keep["x_dram"][bass.ds(b, 1)].rearrange("a p t -> (a p) t"), x_res[p][:]).then_inc(x_stored[p], 16)
                pool.wait_ge(x_stored[p], i * 16 + 16)
                if load:
                    load_x(pool, b + 2, p)

            @block.gpsimd
            def _(pool):
                for p in two:
                    load_x(pool, p, p)
                with pool.Fori(0, B // 2 - 1) as i:
                    for p in two:
                        residual(pool, i * 2 + p, p, i, True)
                for p in two:
                    residual(pool, B - 2 + p, p, B // 2 - 1, False)


def feed_forward(nc, d, keep):
    with ExitStack() as ctx:
        sb = lambda name, shape, dt: ctx.enter_context(nc.sbuf_tensor(name, shape, dt))
        ps = lambda name, shape, dt: ctx.enter_context(nc.psum_tensor(name, shape, dt))
        sem = lambda name: ctx.enter_context(nc.semaphore(name))
        two = range(2)
        groups = B // GROUP
        xg = [sb(f"xg{p}", [P, GROUP, T], F32) for p in two]
        xn = sb("xn_ffn", [P, GROUP, T], F32)
        stats = sb("stats_ffn", [P, GROUP, 6], F32)
        moments = sb("moments_ffn", [P, GROUP, 2], F32)
        rstd = sb("rstd_ffn", [P, 2, GROUP], F32)
        eps = sb("eps_ffn", [P, 2], F32)
        x_head = sb("x_head", [P, KT, T], F32R)
        x_rest = sb("x_rest", [P, KT, T], F32R)
        x_bf16 = sb("x_bf16", [P, KT, T], BF16)
        silu = [sb(f"silu{p}", [P, T], F32) for p in two]
        hidden = [sb(f"hidden{p}", [P, T], F32) for p in two]
        h_head = [sb(f"h_head{p}", [P, T], F32R) for p in two]
        h_rest = [sb(f"h_rest{p}", [P, T], F32R) for p in two]
        h_bf16 = [sb(f"h_bf16{p}", [P, T], BF16) for p in two]
        squares = sb("squares", [P, GROUP, T], F32)
        rms = sb("rms", [P, 3, GROUP], F32)
        y_out = [sb(f"y_out{p}", [P, GROUP, T], F32) for p in two]
        gu_ps = [ps(f"gu_ps{p}", [P, 2, T], F32) for p in two]
        y_ps = ps("y_ps", [P, GROUP, T], F32)

        xg_in = [sem(f"xg_in{p}") for p in two]
        consts = sem("consts3")
        stat = sem("stat3")
        dev = sem("dev3")
        inv = sem("inv3")
        normed = sem("normed3")
        turned = sem("turned3")
        heads = sem("heads3")
        rests = sem("rests3")
        gu_done = sem("gu_done")
        silu_ok = sem("silu_ok")
        hid_ok = sem("hid_ok")
        h_heads = sem("h_heads")
        h_rests = sem("h_rests")
        h_bf16s = sem("h_bf16s")
        down = sem("down")
        squared = sem("squared")
        rooted = sem("rooted")
        scaled = sem("scaled3")
        y_ok = sem("y_ok")
        stored = [sem(f"stored3{p}") for p in two]

        with nc.Block() as block:
            @block.sync
            def _(sp):
                def load(g, p):
                    sp.dma_start(xg[p][:], keep["x_dram"][bass.ds(g * GROUP, GROUP)].rearrange("j p t -> p j t")).then_inc(xg_in[p], 16)

                def store(g, p):
                    sp.wait_ge(y_ok, g * GROUP + GROUP)
                    sp.dma_start(d["out"][bass.ds(g * GROUP, GROUP)].rearrange("j p t -> p j t"), y_out[p][:]).then_inc(stored[p], 16)

                for p in two:
                    load(p, p)
                with sp.Fori(0, groups // 2 - 1) as i:
                    for p in two:
                        g = i * 2 + p
                        store(g, p)
                        load(g + 2, p)
                for p in two:
                    store(groups - 2 + p, p)
                for p in two:
                    sp.wait_ge(stored[p], 16 * (groups // 2))

            def normalise(dve, g, i, p):
                dve.wait_ge(xg_in[p], i * 16 + 16)
                for j in range(GROUP):
                    nc.vector.bn_stats(stats[:, j, :], xg[p][:, j, :]).then_inc(stat, 1)
                for j in range(GROUP):
                    dve.wait_ge(stat, g * 8 + j + 1)
                    nc.vector.bn_aggr(moments[:, j, :], stats[:, j, :]).then_inc(stat, 1)
                dve.wait_ge(dev, g + 1)
                nc.vector.reciprocal(rstd[:, 1, :], rstd[:, 0, :]).then_inc(inv, 1)
                dve.wait_ge(inv, g + 1)
                for j in range(GROUP):
                    nc.vector.tensor_scalar(xn[:, j, :], xg[p][:, j, :], moments[:, j, 0:1], rstd[:, 1, j:j + 1],
                                            ALU.subtract, ALU.mult).then_inc(normed, 1)

            def vector_group(dve, i, p, last):
                g = i * 2 + p
                for k in range(KT):
                    dve.wait_ge(heads, g * 8 + 2 * k + 2)
                    nc.vector.tensor_tensor(x_rest[:, k], gu_ps[k // 2][:, k % 2], x_head[:, k].bitcast(F32),
                                            ALU.subtract).then_inc(rests, 1)
                for t in range(IT):
                    at = g * IT + t
                    dve.wait_ge(silu_ok, at + 1)
                    if not (isinstance(g, int) and g == 0 and t < 2):
                        dve.wait_ge(h_bf16s, at - 1)
                    nc.vector.tensor_tensor(hidden[t % 2][:], gu_ps[t % 2][:, 1], silu[t % 2][:], ALU.mult).then_inc(hid_ok, 1)
                    dve.wait_ge(h_heads, at + 1)
                    nc.vector.tensor_tensor(h_rest[t % 2][:], hidden[t % 2][:], h_head[t % 2][:].bitcast(F32),
                                            ALU.subtract).then_inc(h_rests, 1)
                    if t == IT // 2 and not last:
                        normalise(dve, g + 1, i + p, 1 - p)
                dve.wait_ge(rooted, g + 1)
                nc.vector.reciprocal(rms[:, 2, :], rms[:, 1, :]).then_inc(scaled, 1)
                dve.wait_ge(scaled, g * 2 + 1)
                nc.vector.tensor_scalar(rms[:, 2, :], rms[:, 2, :], keep["gates"][:, 1:2], None, ALU.mult).then_inc(scaled, 1)
                dve.wait_ge(scaled, g * 2 + 2)
                if not (isinstance(i, int) and i == 0):
                    dve.wait_ge(stored[p], i * 16)
                for j in range(GROUP):
                    nc.vector.scalar_tensor_tensor(y_out[p][:, j, :], y_ps[:, j, :], rms[:, 2, j:j + 1], xg[p][:, j, :],
                                                   ALU.mult, ALU.add).then_inc(y_ok, 1)

            @block.vector
            def _(dve):
                nc.vector.memset(eps[:, 0:1], LN_EPS).then_inc(consts, 1)
                nc.vector.memset(eps[:, 1:2], RMS_EPS).then_inc(consts, 1)
                normalise(dve, 0, 0, 0)
                vector_group(dve, 0, 0, False)
                vector_group(dve, 0, 1, False)
                if groups > 4:
                    with dve.Fori(1, groups // 2 - 1) as i:
                        for p in two:
                            vector_group(dve, i, p, False)
                vector_group(dve, groups // 2 - 1, 0, False)
                vector_group(dve, groups // 2 - 1, 1, True)

            def deviations(act, g):
                act.wait_ge(stat, g * 8 + 8)
                nc.scalar.activation(rstd[:, 0, :], moments[:, :, 1], ACT.Sqrt, bias=eps[:, 0:1]).then_inc(dev, 1)

            def scalar_group(act, g, last):
                for k in range(KT):
                    act.wait_ge(turned, g * KT + k + 1)
                    nc.scalar.activation(x_head[:, k], gu_ps[k // 2][:, k % 2], ACT.Copy).then_inc(heads, 1)
                    nc.scalar.activation(x_bf16[:, k], gu_ps[k // 2][:, k % 2], ACT.Copy).then_inc(heads, 1)
                for t in range(IT):
                    at = g * IT + t
                    act.wait_ge(gu_done, at + 1)
                    nc.scalar.activation(silu[t % 2][:], gu_ps[t % 2][:, 0], ACT.Silu).then_inc(silu_ok, 1)
                    act.wait_ge(hid_ok, at + 1)
                    if not (isinstance(g, int) and g == 0 and t < 2):
                        act.wait_ge(down, at - 1)
                    nc.scalar.activation(h_head[t % 2][:], hidden[t % 2][:], ACT.Copy).then_inc(h_heads, 1)
                    nc.scalar.activation(h_bf16[t % 2][:], hidden[t % 2][:], ACT.Copy).then_inc(h_bf16s, 1)
                    if t == IT // 2 and not last:
                        deviations(act, g + 1)
                act.wait_ge(down, g * IT + IT)
                for j in range(GROUP):
                    nc.scalar.activation(squares[:, j], y_ps[:, j, :], ACT.Square, accum_out=rms[:, 0, j:j + 1]).then_inc(squared, 1)
                act.wait_ge(squared, g * GROUP + GROUP)
                nc.scalar.activation(rms[:, 1, :], rms[:, 0, :], ACT.Sqrt, bias=eps[:, 1:2], scale=1.0 / T).then_inc(rooted, 1)

            @block.scalar
            def _(act):
                act.wait_ge(consts, 2)
                deviations(act, 0)
                scalar_group(act, 0, False)
                with act.Fori(1, groups - 1) as g:
                    scalar_group(act, g, False)
                scalar_group(act, groups - 1, True)

            def gate_up(pe, g, t):
                at = g * IT + t
                if t == 0:
                    pe.wait_ge(heads, g * 8 + 8)
                    pe.wait_ge(rests, g * 4 + 4)
                elif t > 1:
                    pe.wait_ge(hid_ok, at - 1)
                for half, col in ((0, t * P), (1, INNER + t * P)):
                    for k in range(KT):
                        head = keep["gu_head"][:, k, col:col + P]
                        nc.tensor.matmul(gu_ps[t % 2][:, half], head, x_head[:, k], start=(k == 0), stop=False)
                        nc.tensor.matmul(gu_ps[t % 2][:, half], head, x_rest[:, k], start=False, stop=False)
                    for k in range(KT):
                        last = nc.tensor.matmul(gu_ps[t % 2][:, half], keep["gu_rest"][:, k, col:col + P], x_bf16[:, k],
                                                start=False, stop=(k == KT - 1))
                last.then_inc(gu_done, 1)

            def project_down(pe, g, t, first):
                at = g * IT + t
                pe.wait_ge(h_heads, at + 1)
                pe.wait_ge(h_rests, at + 1)
                pe.wait_ge(h_bf16s, at + 1)
                if t == 0 and not first:
                    pe.wait_ge(y_ok, g * GROUP)
                for j in range(GROUP):
                    cols = slice(j * P, (j + 1) * P)
                    for n, (h, w) in enumerate(((h_head, "dn_head"), (h_rest, "dn_head"), (h_bf16, "dn_rest"))):
                        last = nc.tensor.matmul(y_ps[:, j, :], h[t % 2][:, cols], keep[w][:, t, :],
                                                start=(t == 0 and n == 0), stop=(t == IT - 1 and n == 2))
                last.then_inc(down, 1)

            def tensor_group(pe, g, first):
                pe.wait_ge(normed, g * GROUP + GROUP)
                if not first:
                    pe.wait_ge(hid_ok, g * IT)
                for k in range(KT):
                    for j in range(GROUP):
                        last = nc.tensor.transpose(gu_ps[k // 2][:, k % 2, j * P:(j + 1) * P], xn[:, j, k * P:(k + 1) * P],
                                                   keep["ident"][:])
                    last.then_inc(turned, 1)
                for t in range(IT):
                    gate_up(pe, g, t)
                    if t:
                        project_down(pe, g, t - 1, first)
                project_down(pe, g, IT - 1, first)

            @block.tensor
            def _(pe):
                tensor_group(pe, 0, True)
                with pe.Fori(1, groups) as g:
                    tensor_group(pe, g, False)


def build(nc, d):
    with ExitStack() as ctx:
        sb = lambda name, shape, dt: ctx.enter_context(nc.sbuf_tensor(name, shape, dt))
        keep = {
            "ident": sb("ident", [P, P], F32),
            "gates": sb("gates", [P, 2], F32),
            "gu_head": sb("gu_head", [P, KT, 2 * INNER], F32R),
            "gu_rest": sb("gu_rest", [P, KT, 2 * INNER], BF16),
            "dn_head": sb("dn_head", [P, IT, T], F32R),
            "dn_rest": sb("dn_rest", [P, IT, T], BF16),
            "qk_dram": nc.dram_tensor("qk_scratch", [B, 2, HEADS, 2, KC, T], F32).ap(),
            "v_dram": nc.dram_tensor("v_scratch", [B, P, KT * HEADS * 2 * KC], F32).ap(),
            "x_dram": nc.dram_tensor("x_scratch", [B, P, T], F32).ap(),
        }
        unpack_weights(nc, d, keep)
        project(nc, d, keep)
        attend(nc, d, keep)
        feed_forward(nc, d, keep)


def kernel(**inputs):
    import concourse.bacc as bacc
    from concourse.bass_utils import run_bass_kernel_spmd

    a = {k: np.ascontiguousarray(v) for k, v in inputs.items()}
    theta = (1.0 / np.float32(10000.0) ** (np.arange(0, ROT, 2, dtype=np.float32) / np.float32(ROT))).astype(np.float32)
    angle = np.arange(T, dtype=np.float32)[None, :] * np.concatenate([theta, theta])[:, None]
    turn = np.concatenate([-np.ones(ROT // 2, np.float32), np.ones(ROT // 2, np.float32)])[:, None]
    cos = np.concatenate([np.cos(angle), np.ones((KC - ROT, T), np.float32)])
    sin = np.concatenate([np.sin(angle) * turn, np.zeros((KC - ROT, T), np.float32)])
    arrays = {
        "x": a["x"], "ctx": a["ctx_2048"], "g_xattn": a["g_xattn"], "g_ffn": a["g_ffn"],
        "wqT": np.ascontiguousarray(a["L0_xattn_Wq"].T), "wkT": np.ascontiguousarray(a["L0_xattn_Wk"].T),
        "wvT": np.ascontiguousarray(a["L0_xattn_Wv"].T), "woT": np.ascontiguousarray(a["L0_xattn_Wo"].T),
        "bq": a["L0_xattn_bq"], "bk": a["L0_xattn_bk"], "bv": a["L0_xattn_bv"], "bo": a["L0_xattn_bo"],
        "gate_up_packed": a["L0_ffn_gate_up_packed"].view(np.uint32), "gate_up_scales": a["L0_ffn_gate_up_scales"],
        "down_packed": a["L0_ffn_down_packed"].view(np.uint32), "down_scales": a["L0_ffn_down_scales"],
        "cos": np.tile(cos, (HEADS, 1)).astype(np.float32), "sin": np.tile(sin, (HEADS, 1)).astype(np.float32),
        "ident": np.eye(P, dtype=np.float32),
    }
    nc = bacc.Bacc("TRN2", target_bir_lowering=False, num_devices=1)
    d = {name: nc.dram_tensor(name + "_dram", v.shape, mybir.dt.from_np(v.dtype), kind="ExternalInput").ap()
         for name, v in arrays.items()}
    d["out"] = nc.dram_tensor("out_dram", (B, P, T), F32, kind="ExternalOutput").ap()
    build(nc, d)
    r = run_bass_kernel_spmd(nc, [{name + "_dram": v for name, v in arrays.items()}], core_ids=[0])
    return r.results[0]["out_dram"]
```

```python
from contextlib import ExitStack

import numpy as np

import concourse.bass as bass
from concourse import mybir

ALU = mybir.AluOpType
ACT = mybir.ActivationFunctionType
AXIS_X = mybir.AxisListType.X
F32 = mybir.dt.float32
F32R = mybir.dt.float32r
BF16 = mybir.dt.bfloat16
F16 = mybir.dt.float16
FP8E3 = mybir.dt.float8e3
U32 = mybir.dt.uint32

P = 128
B = 16
T = 512
HEADS = 8
KC = P // HEADS
ROT = KC // 2
KT = T // P
INNER = 1408
IT = INNER // P
GU = 2 * INNER // P
LN_EPS = 1e-5
RMS_EPS = 1e-6
SCORE_SCALE = KC ** -0.5

STACK = 64
PARTS = 3
MAX_ROW = P - 1
QUAD = 4
GROUP = 4


GU_WORDS, DN_WORDS = GU * T // 8, KT * INNER // 8
WORDS = GU_WORDS + DN_WORDS
PIECES = (slice(0, GU_WORDS // 2), slice(GU_WORDS // 2, GU_WORDS), slice(GU_WORDS, WORDS))


UNITS = 4
RING = 3
TILES = HEADS * KT
PER_SLOT = TILES // (UNITS * QUAD)
HALF_LOADS = 10
SPLIT_STORES = 2


def score_tiles(unit, slot):
    ahead, n = (2, 0) if unit == UNITS - 1 else (1, unit + 1)
    first = (n * QUAD + slot) * PER_SLOT
    return ahead, list(range(first, first + PER_SLOT))


def bank_before(at, n):
    return at - (RING if n >= RING else TILES - max(m for m in range(TILES) if m % RING == n) + n)


def turn_of(b, p):
    return b // 2 if isinstance(b, int) else (b - p) // 2


def attend(nc, d, keep):
    with ExitStack() as ctx:
        sb = lambda name, shape, dt: ctx.enter_context(nc.sbuf_tensor(name, shape, dt))
        ps = lambda name, shape, dt: ctx.enter_context(nc.psum_tensor(name, shape, dt))
        sem = lambda name: ctx.enter_context(nc.semaphore(name))
        two = range(2)
        halves = (slice(0, P // 2), slice(P // 2, P))
        wq, wk, wv = (sb(n, [P, P], F32) for n in ("wq", "wk", "wv"))
        bias = sb("qk_bias", [P, 2], F32)
        scale = sb("qk_scale", [P, 1], F32)
        bias_v = sb("bias_v", [P, P], F32)
        eps = sb("ln_eps", [P, 1], F32)
        cos, sin = sb("cos", [P, T], F32), sb("sin", [P, T], F32)
        xt = [sb(f"xt{p}", [P, T], F32) for p in two]
        ct = [sb(f"ct{p}", [P, T], F32) for p in two]
        cv = sb("cv", [P, T], F32)
        xn = [sb(f"xn{p}", [P, T], F32) for p in two]
        stats = [sb(f"stats{p}", [P, 6], F32) for p in two]
        moments = [sb(f"moments{p}", [P, 2], F32) for p in two]
        rstd = [sb(f"rstd{p}", [P, 2], F32) for p in two]
        proj = [sb(f"proj{p}", [P, 2, T], F32) for p in two]
        swap = [sb(f"swap{p}", [P, T], F32) for p in two]
        split = [sb(f"split{p}", [P, 2, 2, T], F32R) for p in two]
        q_stack = [sb(f"q_stack{p}", [P, HEADS, T], F32R) for p in two]
        k_stack = [sb(f"k_stack{p}", [P, HEADS // 2, T], F32R) for p in two]
        v_ones = [sb(f"v_ones{p}", [P, KT, HEADS, 2 * KC], F32) for p in two]
        x_res = [sb(f"x_res{p}", [P, T], F32) for p in two]
        probs = [sb(f"probs{p}", [P, QUAD, 2, T], F32) for p in two]
        row_max = [sb(f"row_max{p}", [P, HEADS, KT], F32) for p in two]
        neg_max = [sb(f"neg_max{p}", [HEADS * KT, P], F32R) for p in two]
        sums_of = sb("pv_sb", [P, T], F32)
        scale_of = sb("scale_of", [P, T], F32)
        heads_out = [sb(f"heads_out{q}", [P, T], F32) for q in two]
        attn = sb("attn", [P, T], F32)
        wo = [sb(f"wo{q}", [P, P], F32) for q in two]
        bias_o, gate_bias = sb("bias_o", [P, 1], F32), sb("gate_bias", [P, 1], F32)
        gate_in = sb("gate_in", [P, 2], F32)

        part_a, part_b = (sb(n, [P, WORDS], U32) for n in ("part_a", "part_b"))
        packed, sign = (probs[p][:].rearrange("p h k t -> p (h k t)").bitcast(U32)[:, 0:WORDS] for p in two)
        gu_sc16 = sb("gu_sc16", [KT * GU, P], F16)
        dn_sc16 = sb("dn_sc16", [IT * KT, P], F16)
        gu_sc32 = sb("gu_sc32", [KT * GU, P], F32)
        dn_sc32 = sb("dn_sc32", [IT * KT, P], F32)

        st_ps = [ps(f"st_ps{r}", [P, T], F32) for r in range(RING)]
        s_ps = [ps(f"s_ps{r}", [P, T], F32) for r in range(RING)]
        pv_ps = ps("pv_ps", [P, T], F32)
        first_banks = [(st_ps[0], st_ps[1]), (st_ps[2], s_ps[0]), (st_ps[0], st_ps[1])]
        misc_ps = ps("misc_ps", [P, T], F32)

        gates_in = sem("gates_in")
        weights_in = sem("weights_in")
        const_in = sem("const_in")
        wo_in = sem("wo_in")
        packed_in = [sem(f"packed_in_{piece}") for piece in ("gate", "up", "down")]
        scales_in = sem("scales_in")
        bits = sem("bits")
        scales_f32 = sem("scales_f32")
        scales_t = sem("scales_t")
        scales_ok = sem("scales_ok")
        vals_ok = sem("vals_ok")
        blank = sem("blank")
        consts = sem("consts")
        gated = sem("gated")
        loaded = [sem(f"loaded{p}") for p in two]
        cv_in = sem("cv_in")
        stat = sem("stat")
        var_log = sem("var_log")
        dev = sem("dev")
        normed = sem("normed")
        rot_done = sem("rot_done")
        pass_done = sem("pass_done")
        v_done = sem("v_done")
        biased = sem("biased")
        swapped = sem("swapped")
        cosine = sem("cosine")
        sine = sem("sine")
        rotated = sem("rotated")
        heads = sem("heads1")
        rests = sem("rests1")
        stored = [sem(f"stored{p}") for p in two]
        v_ready = sem("v_ready")
        half_in = [[sem(f"half_in{p}{h}") for h in two] for p in two]
        x_in = [sem(f"x_in{p}") for p in two]
        scored = sem("scored")
        maxed = sem("maxed")
        max_turned = sem("max_turned")
        max_neg = sem("max_neg")
        max_in = [sem(f"max_in{p}") for p in two]
        st_done = sem("st_done")
        expd = sem("expd")
        pv_done = sem("pv_done")
        pv_out = sem("pv_out")
        passed = sem("passed")
        sums_up = sem("sums_up")
        logs = sem("logs")
        inverses = sem("inverses")
        quad_done = sem("quad_done")
        mixed = sem("mixed")
        attn_ok = sem("attn_ok")
        x_ok = sem("x_ok")
        x_stored = [sem(f"x_stored{p}") for p in two]
        spread = [KC + i % KC for i in range(32)]
        partner = [(i // ROT) * ROT + (i + ROT // 2) % ROT for i in range(32)]
        WEIGHTS, CONSTS, WO, BLANKS = 16 * 3, 16 * 6, 16 * 2 * QUAD, 6
        CONSTS_BIAS, CONSTS_ONES, CONSTS_ALL = 5, 7, 8
        half = IT // 2
        parts_of_values = [(vals, rows, part_of, piece, odd) for odd in two for vals, rows, part_of, piece in (
            (keep["gu_vals"], slice(0, half), IT, 0), (keep["gu_vals"], slice(half, IT), IT, 0),
            (keep["gu_vals"], slice(IT, IT + half), IT, 1), (keep["gu_vals"], slice(IT + half, GU), IT, 1),
            (keep["dn_vals"], slice(0, KT // 2), KT, 2), (keep["dn_vals"], slice(KT // 2, KT), KT, 2))]
        starting = lambda b, n: isinstance(b, int) and b < n

        with nc.Block() as block:
            def load_inputs(sp, b, p):
                sp.dma_start(xt[p][:], d["x"][bass.ds(b, 1)].rearrange("a p t -> (a p) t")).then_inc(loaded[p], 16)
                sp.dma_start(ct[p][:], d["ctx"][bass.ds(b, 1)].rearrange("a p t -> (a p) t")).then_inc(loaded[p], 16)

            def load_cv(sp, b):
                sp.dma_start(cv[:], d["ctx"][bass.ds(b, 1)].rearrange("a p t -> (a p) t")).then_inc(cv_in, 16)

            def store_split(sp, b, p):
                sp.wait_ge(rests, 2 * b + 2)
                for w in two:
                    rows = keep["qk_dram"][bass.ds(b, 1), :, :, w * ROT:(w + 1) * ROT].rearrange("a q h c s t -> (a q h) c (s t)")
                    sp.dma_start(rows, split[p][:, w].bitcast(F32).rearrange("p s t -> p (s t)")).then_inc(stored[p], 16)

            def load_half(sp, b, p, h):
                sp.wait_ge(stored[p], turn_of(b, p) * 16 * SPLIT_STORES + 16 * SPLIT_STORES)
                slots = slice(2 * h, 2 * h + 2)
                both = slice(0, 2 * KC)
                for stack, which, parts in ((q_stack, 0, ((0, 1, both), (2 * KC, 1, slice(0, 2 * KC, 2)))),
                                            (k_stack, 1, ((0, 2, slice(0, 2 * KC, 2)), (1, 2, slice(0, 2 * KC, 2)),
                                                          (2 * KC, 1, slice(1, 2 * KC, 2))))):
                    src = keep["qk_dram"][bass.ds(b, 1), which].rearrange("a (j two) c s t -> two (a c s) j t", two=2)
                    for odd in two:
                        for row, step, take in parts:
                            n = len(range(2 * KC)[take])
                            at = STACK * odd + row
                            rows = stack[p][at:at + (n - 1) * step + 1:step, :, :].bitcast(F32)
                            if which == 0:
                                rows = rows.rearrange("c (j two) t -> c j two t", two=2)[:, :, odd, :]
                            sp.dma_start(rows[:, slots, :], src[odd, take, slots, :]).then_inc(half_in[p][h], 16)

            def load_max(sp, b, p):
                sp.wait_ge(max_neg, b + 1)
                sp.dma_start(q_stack[p][MAX_ROW:MAX_ROW + 1, :, :].bitcast(F32).rearrange("a h t -> a (h t)"),
                             neg_max[p][:].bitcast(F32)).then_inc(max_in[p], 16)

            def load_x(sp, b, p):
                sp.dma_start(x_res[p][:], d["x"][bass.ds(b, 1)].rearrange("a p t -> (a p) t")).then_inc(x_in[p], 16)

            def store_x(sp, b, p):
                sp.wait_ge(x_ok, b + 1)
                sp.dma_start(keep["x_dram"][bass.ds(b, 1)].rearrange("a p t -> (a p) t"), x_res[p][:]).then_inc(x_stored[p], 16)

            def sync_step(sp, b, p, left):
                if left and not starting(b, 1):
                    sp.wait_ge(st_done, b * TILES)
                    load_half(sp, b + 1, 1 - p, 1)
                if left:
                    sp.wait_ge(v_done, b + 1)
                    load_cv(sp, b + 1)
                if left >= 4:
                    sp.wait_ge(pass_done, b + 3)
                    load_inputs(sp, b + 4, p)
                if not starting(b, 2):
                    store_x(sp, b - 2, p)
                if left >= 2:
                    sp.wait_ge(st_done, b * TILES + TILES // 2)
                    load_half(sp, b + 2, p, 0)
                if left >= 3:
                    store_split(sp, b + 3, 1 - p)
                if not starting(b, 2):
                    sp.wait_ge(x_stored[p], turn_of(b, p) * 16)
                    load_x(sp, b, p)
                if left:
                    load_max(sp, b + 1, 1 - p)

            @block.sync
            def _(sp):
                load_inputs(sp, 0, 0)
                for n, name in enumerate(("g_xattn", "g_ffn")):
                    sp.dma_start(gate_in[:, n:n + 1], d[name].rearrange("(a n) -> a n", a=1).to_broadcast([P, 1])).then_inc(gates_in, 16)
                for out, name in ((wq, "wqT"), (wk, "wkT"), (bias, "qk_bias")):
                    sp.dma_start(out[:], d[name]).then_inc(weights_in, 16)
                load_inputs(sp, 1, 1)
                for out, name in ((cos, "cos"), (sin, "sin"), (wv, "wvT"), (keep["ident"], "ident")):
                    sp.dma_start(out[:], d[name]).then_inc(const_in, 16)
                sp.dma_start(bias_v[:], d["bv"].rearrange("(a n) -> a n", a=1).to_broadcast([P, P])).then_inc(const_in, 16)
                sp.dma_start(bias_o[:], d["bo"].rearrange("(p a) -> p a", a=1)).then_inc(const_in, 16)
                load_cv(sp, 0)
                for b in two:
                    sp.wait_ge(pass_done, b + 1)
                    load_inputs(sp, b + 2, b)
                for n in range(2):
                    rows = slice(n * INNER, (n + 1) * INNER)
                    sp.dma_start(packed[:, PIECES[n]].rearrange("p (t w) -> p t w", t=IT),
                                 d["gate_up_packed"][rows, :].rearrange("(t p) w -> p t w", p=P)).then_inc(packed_in[n], 16)
                sp.dma_start(packed[:, PIECES[2]].rearrange("p (t w) -> p t w", t=KT),
                             d["down_packed"].rearrange("(t p) w -> p t w", p=P)).then_inc(packed_in[2], 16)
                sp.dma_start(gu_sc16[:], d["gate_up_scales"].rearrange("g (t o) -> (g t) o", o=P)).then_inc(scales_in, 16)
                sp.dma_start(dn_sc16[:], d["down_scales"].rearrange("g (t o) -> (g t) o", o=P)).then_inc(scales_in, 16)
                sp.wait_ge(blank, BLANKS)
                store_split(sp, 0, 0)
                for h in two:
                    load_half(sp, 0, 0, h)
                store_split(sp, 1, 1)
                for h in two:
                    load_half(sp, 1, 1, h)
                store_split(sp, 2, 0)
                for q in two:
                    for j in range(QUAD):
                        rows = slice((q * QUAD + j) * KC, (q * QUAD + j + 1) * KC)
                        sp.dma_start(wo[q][2 * KC * j:2 * KC * j + KC, :], d["woT"][rows, :]).then_inc(wo_in, 16)
                for b in two:
                    load_x(sp, b, b)
                load_max(sp, 0, 0)
                for b in two:
                    sync_step(sp, b, b, B - 1 - b)
                with sp.Fori(1, B // 2 - 2) as i:
                    for p in two:
                        sync_step(sp, i * 2 + p, p, 4)
                for b in range(B - 4, B):
                    sync_step(sp, b, b % 2, B - 1 - b)
                for b in (B - 2, B - 1):
                    store_x(sp, b, b % 2)
                for p in two:
                    sp.wait_ge(x_stored[p], 16 * (B // 2))

            def project_rot(pe, n, p, out):
                pe.wait_ge(normed, n + 1)
                pe.wait_ge(loaded[p], turn_of(n, p) * 32 + 32)
                for rows, w, x in ((halves[0], wq, xn), (halves[1], wk, ct)):
                    last = nc.tensor.matmul(out[rows], w[:, halves[0]], x[p][:], start=True, stop=True)
                last.then_inc(rot_done, 1)

            def project_pass(pe, n, p, out):
                for rows, w, x in ((halves[0], wq, xn), (halves[1], wk, ct)):
                    last = nc.tensor.matmul(out[rows], w[:, halves[1]], x[p][:], start=True, stop=True)
                last.then_inc(pass_done, 1)

            def project_v(pe, b):
                pe.wait_ge(cv_in, b * 16 + 16)
                for k in range(KT):
                    last = nc.tensor.matmul(misc_ps[:, k * P:(k + 1) * P], cv[:, k * P:(k + 1) * P], wv[:], start=True, stop=True)
                last.then_inc(v_done, 1)

            def score(pe, b, p, tiles):
                rows = slice(0, MAX_ROW)
                for n in tiles:
                    head, qt = n // KT, n % KT
                    at = b * TILES + n
                    if n % (TILES // 2) == 0:
                        pe.wait_ge(half_in[p][n // (TILES // 2)], turn_of(b, p) * 16 * HALF_LOADS + 16 * HALF_LOADS)
                    if not (starting(b, 1) and n < RING):
                        pe.wait_ge(maxed, bank_before(at, n) + 1)
                    nc.tensor.matmul(s_ps[n % RING][:], q_stack[p][rows, head, qt * P:(qt + 1) * P],
                                     k_stack[p][rows, head // 2, :], start=True, stop=True).then_inc(scored, 1)

            def turn_max(pe, b, p):
                pe.wait_ge(maxed, b * TILES + TILES)
                pe.wait_ge(v_ready, b + 1)
                nc.tensor.transpose(misc_ps[0:HEADS * KT, 0:P], row_max[p][:].rearrange("p h k -> p (h k)"),
                                    keep["ident"][:]).then_inc(max_turned, 1)

            def values(pe, b, p, half, part):
                quad = half // 2
                at = b * UNITS + half
                kt = 2 * (half % 2) + part
                if part == 0:
                    pe.wait_ge(expd, (at + 1) * 2 * QUAD)
                    if half == 0:
                        pe.wait_ge(v_ready, b + 1)
                    if half % 2 == 0 and not (starting(b, 1) and quad == 0):
                        pe.wait_ge(pv_out, b * 2 + quad)
                for j in range(QUAD):
                    last = nc.tensor.matmul(pv_ps[2 * KC * j:2 * KC * (j + 1), :], v_ones[p][:, kt, quad * QUAD + j, :],
                                            probs[half % 2][:, j, part, :], start=(kt == 0), stop=(kt == KT - 1))
                if part == 1:
                    last.then_inc(pv_done, 1)

            def mix(pe, b):
                pe.wait_ge(quad_done, b * 2 + 2)
                for q in two:
                    last = nc.tensor.matmul(misc_ps[:], wo[q][:], heads_out[q][:], start=(q == 0), stop=(q == 1))
                last.then_inc(mixed, 1)

            def misc_free(pe, b):
                if starting(b, 2):
                    pe.wait_ge(max_neg, b + 1)
                else:
                    pe.wait_ge(attn_ok, b - 1)

            def tensor_step(pe, b, p, left):
                for unit in range(UNITS):
                    for slot in range(QUAD):
                        ahead, tiles = score_tiles(unit, slot)
                        if ahead > left:
                            tiles = []
                        score(pe, b + ahead, (p + ahead) % 2, tiles[:1])
                        if unit == 0 and slot == 0:
                            pe.wait_ge(max_in[p], turn_of(b, p) * 16 + 16)
                        head = (unit // 2) * QUAD + slot
                        for k in range(2):
                            n = 2 * (unit * QUAD + slot) + k
                            if not (starting(b, 1) and n < RING):
                                pe.wait_ge(expd, bank_before(b * TILES + n, n) + 1)
                            kt = 2 * (unit % 2) + k
                            nc.tensor.matmul(st_ps[n % RING][:], k_stack[p][:, head // 2, kt * P:(kt + 1) * P],
                                             q_stack[p][:, head, :], start=True, stop=True).then_inc(st_done, 1)
                        score(pe, b + ahead, (p + ahead) % 2, tiles[1:])
                        if unit == UNITS - 1 and slot == 0 and left:
                            turn_max(pe, b + 1, 1 - p)
                        if slot % 2 and unit:
                            values(pe, b, p, unit - 1, slot // 2)
                        elif slot % 2 and not starting(b, 1):
                            values(pe, b - 1, 1 - p, UNITS - 1, slot // 2)
                        if unit == 0 and slot == 1 and left >= 3:
                            misc_free(pe, b)
                            project_rot(pe, b + 3, 1 - p, misc_ps)
                        if unit == 1 and slot == 0 and left >= 3:
                            pe.wait_ge(biased, 2 * b + 7)
                            project_pass(pe, b + 3, 1 - p, misc_ps)
                        if unit == 2 and slot == 0 and left:
                            if left >= 3:
                                pe.wait_ge(heads, 2 * b + 7)
                            else:
                                misc_free(pe, b)
                            project_v(pe, b + 1)
                        if unit == 3 and slot == 2 and not starting(b, 1):
                            if left:
                                pe.wait_ge(max_neg, b + 2)
                            else:
                                misc_free(pe, b)
                            mix(pe, b - 1)

            @block.tensor
            def _(pe):
                pe.wait_ge(weights_in, WEIGHTS)
                for n in range(3):
                    if n == 2:
                        pe.wait_ge(const_in, CONSTS)
                        project_v(pe, 0)
                        pe.wait_ge(heads, 1)
                    project_rot(pe, n, n % 2, first_banks[n][0])
                    project_pass(pe, n, n % 2, first_banks[n][1])
                pe.wait_ge(scales_f32, 2)
                nc.tensor.transpose(pv_ps[:, 0:KT * GU], gu_sc32[:], keep["ident"][0:KT * GU, 0:KT * GU]).then_inc(scales_t, 1)
                nc.tensor.transpose(pv_ps[:, KT * GU:KT * GU + IT * KT], dn_sc32[:],
                                    keep["ident"][0:IT * KT, 0:IT * KT]).then_inc(scales_t, 1)
                pe.wait_ge(heads, 5)
                score(pe, 0, 0, range(TILES))
                turn_max(pe, 0, 0)
                score(pe, 1, 1, range(TILES // UNITS))
                pe.wait_ge(wo_in, WO)
                pe.wait_ge(scales_ok, 2)
                for b in two:
                    tensor_step(pe, b, b, B - 1 - b)
                with pe.Fori(1, B // 2 - 2) as i:
                    for p in two:
                        tensor_step(pe, i * 2 + p, p, 4)
                for b in range(B - 4, B):
                    tensor_step(pe, b, b % 2, B - 1 - b)
                for part in range(2):
                    values(pe, B - 1, 1, UNITS - 1, part)
                pe.wait_ge(attn_ok, B - 1)
                mix(pe, B - 1)

            def inverse_dev(act, n, p):
                act.wait_ge(stat, n * 2 + 2)
                nc.scalar.activation(rstd[p][:, 0:1], moments[p][:, 1:2], ACT.Ln, bias=eps[:]).then_inc(var_log, 1)
                act.wait_ge(var_log, n + 1)
                nc.scalar.activation(rstd[p][:, 1:2], rstd[p][:, 0:1], ACT.Exp, scale=-0.5).then_inc(dev, 1)

            def bias_rot(act, n, p, rot_ps):
                act.wait_ge(rot_done, n + 1)
                nc.scalar.activation(proj[p][:, 0], rot_ps, ACT.Identity, bias=bias[:, 0:1], scale=scale[:]).then_inc(biased, 1)

            def bias_pass(act, n, p, pass_ps):
                act.wait_ge(pass_done, n + 1)
                if not starting(n, 2):
                    act.wait_ge(rests, n * 2 - 3)
                nc.scalar.activation(proj[p][:, 1], pass_ps, ACT.Identity, bias=bias[:, 1:2], scale=scale[:]).then_inc(biased, 1)

            def head_pass(act, n, p, pass_ps):
                if not starting(n, 2):
                    act.wait_ge(stored[p], turn_of(n, p) * 16 * SPLIT_STORES)
                nc.scalar.activation(split[p][:, 1, 0], pass_ps, ACT.Identity, bias=bias[:, 1:2], scale=scale[:]).then_inc(heads, 1)

            def head_rot(act, n, p):
                act.wait_ge(rotated, n + 1)
                nc.scalar.activation(split[p][:, 0, 0], swap[p][:], ACT.Copy).then_inc(heads, 1)

            def quad_out(act, b, quad):
                act.wait_ge(pv_done, b * UNITS + 2 * quad + 2)
                if not (starting(b, 1) and quad == 0):
                    act.wait_ge(quad_done, b * 2 + quad)
                nc.scalar.activation(sums_of[:], pv_ps[:], ACT.Copy).then_inc(pv_out, 1)

            def quad_inverse(act, b, quad):
                act.wait_ge(sums_up, b * 2 + quad + 1)
                nc.scalar.activation(scale_of[:], scale_of[:], ACT.Ln).then_inc(logs, 1)
                act.wait_ge(logs, b * 2 + quad + 1)
                nc.scalar.activation(scale_of[:], scale_of[:], ACT.Exp, scale=-1.0).then_inc(inverses, 1)

            def gate(act, b):
                act.wait_ge(mixed, b + 1)
                if not starting(b, 1):
                    act.wait_ge(x_ok, b)
                nc.scalar.activation(attn[:], misc_ps[:], ACT.Identity, bias=gate_bias[:], scale=keep["gates"][:, 0:1]).then_inc(attn_ok, 1)

            def scalar_step(act, b, p, left):
                first = starting(b, 1)
                for unit in range(UNITS):
                    done = (b - 1, 1) if unit == 1 else (b, 0)
                    for slot in range(QUAD):
                        if slot == 0 and unit % 2 and not (first and unit == 1):
                            quad_out(act, *done)
                        for k in range(2):
                            n = 2 * (unit * QUAD + slot) + k
                            act.wait_ge(st_done, b * TILES + n + 1)
                            if slot == 0 and k == 0 and not (first and unit < 2):
                                act.wait_ge(pv_done, b * UNITS + unit - 1)
                            nc.scalar.activation(probs[unit % 2][:, slot, k], st_ps[n % RING][:], ACT.Exp).then_inc(expd, 1)
                        if left >= 3:
                            if unit == 0 and slot == 2:
                                bias_rot(act, b + 3, 1 - p, misc_ps[:])
                            if unit == 1 and slot == 1:
                                bias_pass(act, b + 3, 1 - p, misc_ps[:])
                            if unit == 1 and slot == 2:
                                head_pass(act, b + 3, 1 - p, misc_ps[:])
                            if unit == 2 and slot == 0:
                                head_rot(act, b + 3, 1 - p)
                        if left >= 4 and unit == 2 and slot == 1:
                            inverse_dev(act, b + 4, p)
                        if slot == (3 if unit == 1 else 2) and unit % 2 and not (first and unit == 1):
                            quad_inverse(act, *done)
                        if slot == 3 and unit == 3 and not first:
                            gate(act, b - 1)

            @block.scalar
            def _(act):
                act.wait_ge(gates_in, 32)
                nc.scalar.activation(keep["gates"][:], gate_in[:], ACT.Tanh).then_inc(gated, 1)
                nc.scalar.preload_act_table_set("natural_log_exp_and_others")
                act.wait_ge(consts, CONSTS_BIAS)
                for n in two:
                    inverse_dev(act, n, n)
                for n in range(3):
                    bias_rot(act, n, n % 2, first_banks[n][0][:])
                    bias_pass(act, n, n % 2, first_banks[n][1][:])
                    head_pass(act, n, n % 2, first_banks[n][1][:])
                    head_rot(act, n, n % 2)
                    if n < 2:
                        inverse_dev(act, n + 2, n)
                act.wait_ge(scales_in, 32)
                nc.scalar.activation(gu_sc32[:], gu_sc16[:], ACT.Copy, scale=4.0).then_inc(scales_f32, 1)
                nc.scalar.activation(dn_sc32[:], dn_sc16[:], ACT.Copy, scale=4.0).then_inc(scales_f32, 1)
                act.wait_ge(consts, CONSTS_ALL)
                act.wait_ge(bits, 6 * len(PIECES))
                for b in two:
                    scalar_step(act, b, b, B - 1 - b)
                with act.Fori(1, B // 2 - 2) as i:
                    for p in two:
                        scalar_step(act, i * 2 + p, p, 4)
                for b in range(B - 4, B):
                    scalar_step(act, b, b % 2, B - 1 - b)
                quad_out(act, B - 1, 1)
                quad_inverse(act, B - 1, 1)
                gate(act, B - 1)

            def statistics(dve, n, p):
                dve.wait_ge(loaded[p], turn_of(n, p) * 32 + 32)
                nc.vector.bn_stats(stats[p][:], xt[p][:]).then_inc(stat, 1)
                dve.wait_ge(stat, n * 2 + 1)
                dve.sem_inc(passed, 1)
                nc.vector.bn_aggr(moments[p][:], stats[p][:]).then_inc(stat, 1)

            def normalise(dve, n, p):
                dve.wait_ge(dev, n + 1)
                if not starting(n, 2):
                    dve.wait_ge(pass_done, n - 1)
                nc.vector.tensor_scalar(xn[p][:], xt[p][:], moments[p][:, 0:1], rstd[p][:, 1:2], ALU.subtract,
                                        ALU.mult).then_inc(normed, 1)

            def find_partners(dve, n, p):
                dve.wait_ge(biased, n * 2 + 1)
                if not starting(n, 2):
                    dve.wait_ge(rests, n * 2 - 2)
                dve.sem_inc(passed, 1)
                nc.vector.stream_shuffle(swap[p][:], proj[p][:, 0], partner).then_inc(swapped, 1)

            def take_v(dve, b, p):
                dve.wait_ge(v_done, b + 1)
                if not starting(b, 2):
                    dve.wait_ge(pv_done, b * UNITS - UNITS)
                nc.vector.tensor_tensor(v_ones[p][:, :, :, 0:KC], misc_ps[:].rearrange("p (k h c) -> p k h c", k=KT, c=KC),
                                        bias_v[:].rearrange("p (h c) -> p h c", c=KC).unsqueeze(1).to_broadcast([P, KT, HEADS, KC]),
                                        ALU.add).then_inc(v_ready, 1)

            def maxima(dve, b, p, tiles):
                for n in tiles:
                    head, qt = n // KT, n % KT
                    dve.wait_ge(scored, b * TILES + n + 1)
                    if n == 0 and not starting(b, 2):
                        dve.wait_ge(max_turned, b - 1)
                    nc.vector.tensor_reduce(row_max[p][:, head, qt:qt + 1], s_ps[n % RING][:], AXIS_X,
                                            ALU.max).then_inc(maxed, 1)

            def negate(dve, b, p):
                dve.wait_ge(max_turned, b + 1)
                if not starting(b, 2):
                    dve.wait_ge(max_in[p], turn_of(b, p) * 16)
                nc.vector.tensor_scalar(neg_max[p][:], misc_ps[0:HEADS * KT, 0:P], -1.0, None, ALU.mult).then_inc(max_neg, 1)

            def quad_sums(dve, b, quad):
                dve.wait_ge(pv_out, b * 2 + quad + 1)
                dve.sem_inc(passed, 1)
                nc.vector.stream_shuffle(scale_of[:], sums_of[:], spread).then_inc(sums_up, 1)

            def nibble_values(dve, n):
                vals, rows, part_of, piece, odd = parts_of_values[n]
                by = (part_a, part_b)[odd][:, PIECES[piece]].bitcast(FP8E3).rearrange("p (t c) -> p t c", t=part_of)
                first = rows.start - (IT if piece == 1 else 0)
                nc.vector.tensor_copy(vals[:, rows, odd, :], by[:, first:first + rows.stop - rows.start, :]).then_inc(vals_ok, 1)

            def vector_step(dve, b, p, left):
                for unit in range(UNITS):
                    done = (b - 1, 1) if unit == 1 else (b, 0)
                    for slot in range(QUAD):
                        ahead, tiles = score_tiles(unit, slot)
                        if ahead <= left:
                            maxima(dve, b + ahead, (p + ahead) % 2, tiles)
                        if not left and unit * QUAD + slot < len(parts_of_values):
                            nibble_values(dve, unit * QUAD + slot)
                        if unit == 0 and slot == 3 and left >= 3:
                            find_partners(dve, b + 3, 1 - p)
                        if unit % 2 and slot == 0 and not (starting(b, 1) and unit == 1):
                            quad_sums(dve, *done)
                        if unit == 1 and slot == 3 and left >= 4:
                            statistics(dve, b + 4, p)
                        if unit == 2 and slot == 1 and left:
                            take_v(dve, b + 1, 1 - p)
                        if unit == 3 and slot == 0 and left:
                            negate(dve, b + 1, 1 - p)
                        if unit == 3 and slot == 2 and left >= 4:
                            normalise(dve, b + 4, p)

            @block.vector
            def _(dve):
                nc.vector.memset(eps[:], LN_EPS).then_inc(consts, 1)
                nc.vector.memset(scale[halves[0], :], SCORE_SCALE).then_inc(consts, 1)
                nc.vector.memset(scale[halves[1], :], 1.0).then_inc(consts, 1)
                statistics(dve, 0, 0)
                dve.wait_ge(weights_in, WEIGHTS)
                dve.wait_ge(consts, 3)
                for column in two:
                    nc.vector.tensor_scalar(bias[:, column:column + 1], bias[:, column:column + 1], scale[:], None,
                                            ALU.mult).then_inc(consts, 1)
                for p in two:
                    nc.vector.memset(v_ones[p][:], 1.0).then_inc(consts, 1)
                normalise(dve, 0, 0)
                statistics(dve, 1, 1)
                normalise(dve, 1, 1)
                for n in range(3):
                    find_partners(dve, n, n % 2)
                    if n == 0:
                        dve.wait_ge(const_in, CONSTS)
                        dve.wait_ge(consts, CONSTS_ONES)
                        take_v(dve, 0, 0)
                    if n < 2:
                        statistics(dve, n + 2, n)
                        normalise(dve, n + 2, n)
                dve.wait_ge(gated, 1)
                nc.vector.tensor_tensor(gate_bias[:], bias_o[:], keep["gates"][:, 0:1], ALU.mult).then_inc(consts, 1)
                for n, w in enumerate(PIECES):
                    dve.wait_ge(packed_in[n], 16)
                    nc.vector.tensor_scalar(part_a[:, w], packed[:, w], 0x07070707, 3, ALU.bitwise_and,
                                            ALU.logical_shift_left).then_inc(bits, 1)
                    nc.vector.tensor_scalar(sign[:, w], packed[:, w], 0x08080808, 4, ALU.bitwise_and,
                                            ALU.logical_shift_left).then_inc(bits, 1)
                    nc.vector.tensor_scalar(part_b[:, w], packed[:, w], 0x70707070, 1, ALU.bitwise_and,
                                            ALU.logical_shift_right).then_inc(bits, 1)
                    dve.wait_ge(bits, 6 * n + 3)
                    nc.vector.tensor_tensor(part_a[:, w], part_a[:, w], sign[:, w], ALU.bitwise_or).then_inc(bits, 1)
                    nc.vector.tensor_scalar(packed[:, w], packed[:, w], 0x80808080, None, ALU.bitwise_and).then_inc(bits, 1)
                    dve.wait_ge(bits, 6 * n + 5)
                    nc.vector.tensor_tensor(part_b[:, w], part_b[:, w], packed[:, w], ALU.bitwise_or).then_inc(bits, 1)
                dve.wait_ge(scales_t, 2)
                nc.vector.tensor_copy(keep["gu_sc"][:].rearrange("p g t -> p (g t)"), pv_ps[:, 0:KT * GU]).then_inc(scales_ok, 1)
                nc.vector.tensor_copy(keep["dn_sc"][:].rearrange("p g t -> p (g t)"), pv_ps[:, KT * GU:KT * GU + IT * KT]).then_inc(scales_ok, 1)
                maxima(dve, 0, 0, range(TILES))
                negate(dve, 0, 0)
                maxima(dve, 1, 1, range(TILES // UNITS))
                for b in two:
                    vector_step(dve, b, b, B - 1 - b)
                with dve.Fori(1, B // 2 - 2) as i:
                    for p in two:
                        vector_step(dve, i * 2 + p, p, 4)
                for b in range(B - 4, B):
                    vector_step(dve, b, b % 2, B - 1 - b)
                quad_sums(dve, B - 1, 1)

            def rotate(pool, n, p):
                pool.wait_ge(swapped, n + 1)
                nc.gpsimd.tensor_tensor(proj[p][:, 0], proj[p][:, 0], cos[:], ALU.mult).then_inc(cosine, 1)
                nc.gpsimd.tensor_tensor(swap[p][:], swap[p][:], sin[:], ALU.mult).then_inc(sine, 1)
                pool.wait_ge(cosine, n + 1)
                pool.wait_ge(sine, n + 1)
                nc.gpsimd.tensor_tensor(swap[p][:], swap[p][:], proj[p][:, 0], ALU.add).then_inc(rotated, 1)

            def rest_pass(pool, n, p):
                pool.wait_ge(heads, n * 2 + 1)
                nc.gpsimd.tensor_tensor(split[p][:, 1, 1], proj[p][:, 1], split[p][:, 1, 0].bitcast(F32),
                                        ALU.subtract).then_inc(rests, 1)

            def rest_rot(pool, n, p):
                pool.wait_ge(heads, n * 2 + 2)
                nc.gpsimd.tensor_tensor(split[p][:, 0, 1], swap[p][:], split[p][:, 0, 0].bitcast(F32),
                                        ALU.subtract).then_inc(rests, 1)

            def quad_scale(pool, b, quad):
                pool.wait_ge(inverses, b * 2 + quad + 1)
                if not starting(b, 1):
                    pool.wait_ge(mixed, b)
                nc.gpsimd.tensor_tensor(heads_out[quad][:], sums_of[:], scale_of[:], ALU.mult).then_inc(quad_done, 1)

            def residual(pool, b, p):
                pool.wait_ge(x_in[p], turn_of(b, p) * 16 + 16)
                pool.wait_ge(attn_ok, b + 1)
                nc.gpsimd.tensor_tensor(x_res[p][:], x_res[p][:], attn[:], ALU.add).then_inc(x_ok, 1)

            def pool_step(pool, b, p, left):
                if not starting(b, 2):
                    residual(pool, b - 2, p)
                if left >= 3:
                    rotate(pool, b + 3, 1 - p)
                    rest_pass(pool, b + 3, 1 - p)
                if not starting(b, 1):
                    quad_scale(pool, b - 1, 1)
                if left >= 3:
                    rest_rot(pool, b + 3, 1 - p)
                quad_scale(pool, b, 0)

            @block.gpsimd
            def _(pool):
                for tile in wo:
                    nc.gpsimd.memset(tile[:], 0.0).then_inc(blank, 1)
                for tile in q_stack:
                    nc.gpsimd.memset(tile[:].bitcast(F32), 0.0).then_inc(blank, 1)
                for tile in k_stack:
                    nc.gpsimd.memset(tile[:].bitcast(F32), 1.0).then_inc(blank, 1)
                pool.wait_ge(const_in, CONSTS)
                for n in range(3):
                    rotate(pool, n, n % 2)
                    rest_pass(pool, n, n % 2)
                    rest_rot(pool, n, n % 2)
                for b in two:
                    pool_step(pool, b, b, B - 1 - b)
                with pool.Fori(1, B // 2 - 2) as i:
                    for p in two:
                        pool_step(pool, i * 2 + p, p, 4)
                for b in range(B - 4, B):
                    pool_step(pool, b, b % 2, B - 1 - b)
                residual(pool, B - 2, 0)
                quad_scale(pool, B - 1, 1)
                residual(pool, B - 1, 1)


AHEAD = 4
TILES_W = GU + KT * -(-IT // KT)


def feed_forward(nc, d, keep):
    with ExitStack() as ctx:
        sb = lambda name, shape, dt: ctx.enter_context(nc.sbuf_tensor(name, shape, dt))
        ps = lambda name, shape, dt: ctx.enter_context(nc.psum_tensor(name, shape, dt))
        sem = lambda name: ctx.enter_context(nc.semaphore(name))
        two = range(2)
        groups = B // GROUP
        ORDER = [k for bank in ((IT - 2) % 2, (IT - 1) % 2) for k in (2 * bank, 2 * bank + 1)]
        xg = [sb(f"xg{p}", [P, GROUP, T], F32) for p in two]
        xn = sb("xn_ffn", [P, GROUP, T], F32)
        stats = sb("stats_ffn", [P, GROUP, 6], F32)
        moments = sb("moments_ffn", [P, GROUP, 2], F32)
        rstd = sb("rstd_ffn", [P, 2, GROUP], F32)
        eps = sb("eps_ffn", [P, 2], F32)
        x_head = sb("x_head", [P, KT, T], F32R)
        x_rest = sb("x_rest", [P, KT, T], F32R)
        x_bf16 = sb("x_bf16", [P, KT, T], BF16)
        silu = [sb(f"silu{p}", [P, T], F32) for p in two]
        hidden = [sb(f"hidden{p}", [P, T], F32) for p in two]
        h_head = [sb(f"h_head{p}", [P, T], F32R) for p in two]
        h_rest = [sb(f"h_rest{p}", [P, T], F32R) for p in two]
        h_bf16 = [sb(f"h_bf16{p}", [P, T], BF16) for p in two]
        rms = sb("rms", [P, 3, GROUP], F32)
        y_out = sb("y_out", [P, GROUP, T], F32)
        gu_ps = [ps(f"gu_ps{p}", [P, 2, T], F32) for p in two]
        y_ps = ps("y_ps", [P, GROUP, T], F32)

        xg_in = [sem(f"xg_in{p}") for p in two]
        consts = sem("consts3")
        stat = sem("stat3")
        dev = sem("dev3")
        inv = sem("inv3")
        normed = sem("normed3")
        turned = sem("turned3")
        heads = sem("heads3")
        rests = sem("rests3")
        gu_done = sem("gu_done")
        silu_ok = sem("silu_ok")
        hid_ok = sem("hid_ok")
        h_heads = sem("h_heads")
        h_rests = sem("h_rests")
        h_bf16s = sem("h_bf16s")
        down = sem("down")
        squared = sem("squared")
        rooted = sem("rooted")
        scaled = sem("scaled3")
        y_ok = sem("y_ok")
        stored = sem("stored3")
        gu_vals, dn_vals, gu_sc, dn_sc = (keep[n] for n in ("gu_vals", "dn_vals", "gu_sc", "dn_sc"))
        wtile = silu + hidden
        wt_ps = [y_ps[:, p, :].rearrange("p (k o) -> p k o", o=P) for p in range(AHEAD)]
        w_scaled = [sem("w_scaled_dve"), sem("w_scaled_pool")]
        w_turned = sem("w_turned")
        w_heads = sem("w_heads")
        w_rests = sem("w_rests")
        chunks = [(t, g0, min(KT, IT - g0)) for t in range(KT) for g0 in range(0, IT, KT)]
        LOOPED = GU // AHEAD
        STATS, LN, TURN = (LOOPED - 1) * AHEAD, LOOPED * AHEAD, GU + 2

        def source(t):
            if isinstance(t, int) and t >= GU:
                row, g0, n = chunks[t - GU]
                return n, [dn_vals[:, row, o, g0 * 64:(g0 + n) * 64] for o in range(2)], dn_sc[:, g0:g0 + n, row]
            return (KT, [gu_vals[:, bass.ds(t, 1), o, :].rearrange("p a c -> p (a c)") for o in range(2)],
                    gu_sc[:, :, bass.ds(t, 1)].rearrange("p g a -> p (g a)"))

        def place(kind, t):
            if isinstance(t, int) and t >= GU:
                row, g0, n = chunks[t - GU]
                return keep["dn_" + kind][:, g0:g0 + n, row * P:(row + 1) * P]
            return keep["gu_" + kind][:, :, bass.ds(t * P, P)]

        def scale_tile(tensor_tensor, t, p):
            n, vals, scales = source(t)
            for odd in range(2):
                out = wtile[p][:, 0:n * P].rearrange("p (g c two) -> p g c two", g=n, two=2)[:, :, :, odd]
                last = tensor_tensor(out, vals[odd].rearrange("p (g c) -> p g c", g=n),
                                     scales.unsqueeze(2).to_broadcast([P, n, P // 2]), ALU.mult)
            last.then_inc(w_scaled[0 if p == 0 else 1], 1)

        with nc.Block() as block:
            @block.sync
            def _(sp):
                def load(g, p):
                    sp.dma_start(xg[p][:], keep["x_dram"][bass.ds(g * GROUP, GROUP)].rearrange("j p t -> p j t")).then_inc(xg_in[p], 16)

                def store(g):
                    sp.wait_ge(y_ok, g * GROUP + GROUP)
                    sp.dma_start(d["out"][bass.ds(g * GROUP, GROUP)].rearrange("j p t -> p j t"), y_out[:]).then_inc(stored, 16)

                for p in two:
                    load(p, p)
                with sp.Fori(0, groups // 2 - 1) as i:
                    for p in two:
                        g = i * 2 + p
                        store(g)
                        load(g + 2, p)
                for p in two:
                    store(groups - 2 + p)
                sp.wait_ge(stored, 16 * groups)

            def weight_rest(dve, t, p):
                dve.wait_ge(w_heads, t + 1)
                nc.vector.tensor_tensor(place("rest", t), wt_ps[p][:, 0:source(t)[0], :], place("head", t).bitcast(F32),
                                        ALU.subtract).then_inc(w_rests, 1)
                if p == 0 and not (isinstance(t, int) and t + AHEAD >= TILES_W):
                    scale_tile(nc.vector.tensor_tensor, t + AHEAD, p)

            def statistics(dve, g, i, p):
                dve.wait_ge(xg_in[p], i * 16 + 16)
                for j in range(GROUP):
                    nc.vector.bn_stats(stats[:, j, :], xg[p][:, j, :]).then_inc(stat, 1)
                for j in range(GROUP):
                    dve.wait_ge(stat, g * 8 + j + 1)
                    nc.vector.bn_aggr(moments[:, j, :], stats[:, j, :]).then_inc(stat, 1)

            def normalise(dve, g, p):
                dve.wait_ge(dev, g + 1)
                nc.vector.reciprocal(rstd[:, 1, :], rstd[:, 0, :]).then_inc(inv, 1)
                dve.wait_ge(inv, g + 1)
                for j in range(GROUP):
                    nc.vector.tensor_scalar(xn[:, j, :], xg[p][:, j, :], moments[:, j, 0:1], rstd[:, 1, j:j + 1],
                                            ALU.subtract, ALU.mult).then_inc(normed, 1)

            def input_rests(dve, g, part):
                for n in (2 * part, 2 * part + 1):
                    k = ORDER[n]
                    dve.wait_ge(heads, g * 8 + 2 * n + 2)
                    nc.vector.tensor_tensor(x_rest[:, k], gu_ps[k // 2][:, k % 2], x_head[:, k].bitcast(F32),
                                            ALU.subtract).then_inc(rests, 1)

            def vector_group(dve, i, p, last):
                g = i * 2 + p
                for t in range(IT):
                    at = g * IT + t
                    dve.wait_ge(silu_ok, at + 1)
                    if not (isinstance(g, int) and g == 0 and t < 2):
                        dve.wait_ge(h_bf16s, at - 1)
                    nc.vector.tensor_tensor(hidden[t % 2][:], gu_ps[t % 2][:, 1], silu[t % 2][:], ALU.mult).then_inc(hid_ok, 1)
                    dve.wait_ge(h_heads, at + 1)
                    nc.vector.tensor_tensor(h_rest[t % 2][:], hidden[t % 2][:], h_head[t % 2][:].bitcast(F32),
                                            ALU.subtract).then_inc(h_rests, 1)
                    if t == IT // 2 and not last:
                        statistics(dve, g + 1, i + p, 1 - p)
                        normalise(dve, g + 1, 1 - p)
                    if t == IT - 2 and not last:
                        input_rests(dve, g + 1, 0)
                if not last:
                    input_rests(dve, g + 1, 1)
                dve.wait_ge(rooted, g + 1)
                nc.vector.reciprocal(rms[:, 2, :], rms[:, 1, :]).then_inc(scaled, 1)
                dve.wait_ge(scaled, g * 2 + 1)
                nc.vector.tensor_scalar(rms[:, 2, :], rms[:, 2, :], keep["gates"][:, 1:2], None, ALU.mult).then_inc(scaled, 1)
                dve.wait_ge(scaled, g * 2 + 2)
                for j in range(GROUP):
                    nc.vector.scalar_tensor_tensor(y_out[:, j, :], y_ps[:, j, :], rms[:, 2, j:j + 1], xg[p][:, j, :],
                                                   ALU.mult, ALU.add).then_inc(y_ok, 1)

            @block.vector
            def _(dve):
                nc.vector.memset(eps[:, 0:1], LN_EPS).then_inc(consts, 1)
                nc.vector.memset(eps[:, 1:2], RMS_EPS).then_inc(consts, 1)
                scale_tile(nc.vector.tensor_tensor, 0, 0)
                with dve.Fori(0, LOOPED - 1) as i:
                    for p in range(AHEAD):
                        weight_rest(dve, i * AHEAD + p, p)
                for t in range((LOOPED - 1) * AHEAD, TILES_W):
                    if t == STATS:
                        statistics(dve, 0, 0, 0)
                    if t == LN:
                        normalise(dve, 0, 0)
                    if t == TURN:
                        for part in two:
                            input_rests(dve, 0, part)
                    weight_rest(dve, t, t % AHEAD)
                vector_group(dve, 0, 0, False)
                vector_group(dve, 0, 1, False)
                if groups > 4:
                    with dve.Fori(1, groups // 2 - 1) as i:
                        for p in two:
                            vector_group(dve, i, p, False)
                vector_group(dve, groups // 2 - 1, 0, False)
                vector_group(dve, groups // 2 - 1, 1, True)

            def weight_head(act, t, p):
                act.wait_ge(w_turned, t + 1)
                nc.scalar.activation(place("head", t), wt_ps[p][:, 0:source(t)[0], :], ACT.Copy).then_inc(w_heads, 1)

            @block.gpsimd
            def _(pool):
                def step(t, p):
                    if not (isinstance(t, int) and t < AHEAD):
                        pool.wait_ge(w_turned, t - AHEAD + 1)
                    scale_tile(nc.gpsimd.tensor_tensor, t, p)

                for p in range(1, AHEAD):
                    step(p, p)
                with pool.Fori(1, LOOPED) as i:
                    for p in range(1, AHEAD):
                        step(i * AHEAD + p, p)
                for t in range(LOOPED * AHEAD, TILES_W):
                    if t % AHEAD:
                        step(t, t % AHEAD)

            def deviations(act, g):
                act.wait_ge(stat, g * 8 + 8)
                nc.scalar.activation(rstd[:, 0, :], moments[:, :, 1], ACT.Sqrt, bias=eps[:, 0:1]).then_inc(dev, 1)

            def input_heads(act, g, part):
                for n in (2 * part, 2 * part + 1):
                    k = ORDER[n]
                    act.wait_ge(turned, g * KT + n + 1)
                    nc.scalar.activation(x_head[:, k], gu_ps[k // 2][:, k % 2], ACT.Copy).then_inc(heads, 1)
                    nc.scalar.activation(x_bf16[:, k], gu_ps[k // 2][:, k % 2], ACT.Copy).then_inc(heads, 1)

            def scalar_group(act, g, last):
                for t in range(IT):
                    at = g * IT + t
                    act.wait_ge(gu_done, at + 1)
                    nc.scalar.activation(silu[t % 2][:], gu_ps[t % 2][:, 0], ACT.Silu).then_inc(silu_ok, 1)
                    if t == IT - 1 and not last:
                        input_heads(act, g + 1, 0)
                    act.wait_ge(hid_ok, at + 1)
                    if not (isinstance(g, int) and g == 0 and t < 2):
                        act.wait_ge(down, at - 1)
                    nc.scalar.activation(h_head[t % 2][:], hidden[t % 2][:], ACT.Copy).then_inc(h_heads, 1)
                    nc.scalar.activation(h_bf16[t % 2][:], hidden[t % 2][:], ACT.Copy).then_inc(h_bf16s, 1)
                    if t == IT // 2 and not last:
                        deviations(act, g + 1)
                if not last:
                    input_heads(act, g + 1, 1)
                act.wait_ge(down, g * IT + IT)
                if not (isinstance(g, int) and g == 0):
                    act.wait_ge(stored, g * 16)
                for j in range(GROUP):
                    nc.scalar.activation(y_out[:, j], y_ps[:, j, :], ACT.Square, accum_out=rms[:, 0, j:j + 1]).then_inc(squared, 1)
                act.wait_ge(squared, g * GROUP + GROUP)
                nc.scalar.activation(rms[:, 1, :], rms[:, 0, :], ACT.Sqrt, bias=eps[:, 1:2], scale=1.0 / T).then_inc(rooted, 1)

            @block.scalar
            def _(act):
                with act.Fori(0, LOOPED) as i:
                    for p in range(AHEAD):
                        weight_head(act, i * AHEAD + p, p)
                for t in range(LOOPED * AHEAD, TILES_W):
                    if t == LN:
                        act.wait_ge(consts, 2)
                        deviations(act, 0)
                    if t == TURN:
                        for part in two:
                            input_heads(act, 0, part)
                    weight_head(act, t, t % AHEAD)
                scalar_group(act, 0, False)
                with act.Fori(1, groups - 1) as g:
                    scalar_group(act, g, False)
                scalar_group(act, groups - 1, True)

            def turn_weight(pe, t, p):
                rounds = t // AHEAD if isinstance(t, int) else (t - p) // AHEAD
                pe.wait_ge(w_scaled[0 if p == 0 else 1], rounds + 1 if p == 0 else rounds * (AHEAD - 1) + p)
                if not (isinstance(t, int) and t < AHEAD):
                    pe.wait_ge(w_rests, t - AHEAD + 1)
                for k in range(source(t)[0]):
                    last = nc.tensor.transpose(wt_ps[p][:, k, :], wtile[p][:, k * P:(k + 1) * P], keep["ident"][:])
                last.then_inc(w_turned, 1)

            def gate_up(pe, g, t):
                at = g * IT + t
                if t == 0:
                    pe.wait_ge(heads, g * 8 + 8)
                    pe.wait_ge(rests, g * 4 + 4)
                elif t > 1:
                    pe.wait_ge(hid_ok, at - 1)
                for half, col in ((0, t * P), (1, INNER + t * P)):
                    for k in range(KT):
                        head = keep["gu_head"][:, k, col:col + P]
                        nc.tensor.matmul(gu_ps[t % 2][:, half], head, x_head[:, k], start=(k == 0), stop=False)
                        nc.tensor.matmul(gu_ps[t % 2][:, half], head, x_rest[:, k], start=False, stop=False)
                    for k in range(KT):
                        last = nc.tensor.matmul(gu_ps[t % 2][:, half], keep["gu_rest"][:, k, col:col + P], x_bf16[:, k],
                                                start=False, stop=(k == KT - 1))
                last.then_inc(gu_done, 1)

            def project_down(pe, g, t, first):
                at = g * IT + t
                pe.wait_ge(h_heads, at + 1)
                pe.wait_ge(h_rests, at + 1)
                pe.wait_ge(h_bf16s, at + 1)
                if t == 0 and not first:
                    pe.wait_ge(y_ok, g * GROUP)
                for j in range(GROUP):
                    cols = slice(j * P, (j + 1) * P)
                    for n, (h, w) in enumerate(((h_head, "dn_head"), (h_rest, "dn_head"), (h_bf16, "dn_rest"))):
                        last = nc.tensor.matmul(y_ps[:, j, :], h[t % 2][:, cols], keep[w][:, t, :],
                                                start=(t == 0 and n == 0), stop=(t == IT - 1 and n == 2))
                last.then_inc(down, 1)

            def turn_inputs(pe, g, part):
                if part == 0:
                    pe.wait_ge(normed, g * GROUP + GROUP)
                for k in ORDER[2 * part:2 * part + 2]:
                    for j in range(GROUP):
                        last = nc.tensor.transpose(gu_ps[k // 2][:, k % 2, j * P:(j + 1) * P], xn[:, j, k * P:(k + 1) * P],
                                                   keep["ident"][:])
                    last.then_inc(turned, 1)

            def tensor_group(pe, g, first, last):
                for t in range(IT):
                    gate_up(pe, g, t)
                    if t == IT - 1 and not last:
                        pe.wait_ge(hid_ok, g * IT + IT - 1)
                        turn_inputs(pe, g + 1, 0)
                    if t:
                        project_down(pe, g, t - 1, first)
                if not last:
                    pe.wait_ge(hid_ok, g * IT + IT)
                    turn_inputs(pe, g + 1, 1)
                project_down(pe, g, IT - 1, first)

            @block.tensor
            def _(pe):
                for p in range(AHEAD):
                    turn_weight(pe, p, p)
                with pe.Fori(1, LOOPED) as i:
                    for p in range(AHEAD):
                        turn_weight(pe, i * AHEAD + p, p)
                for t in range(LOOPED * AHEAD, TILES_W):
                    if t == TURN:
                        for part in two:
                            turn_inputs(pe, 0, part)
                    turn_weight(pe, t, t % AHEAD)
                pe.wait_ge(w_rests, TILES_W)
                tensor_group(pe, 0, True, False)
                with pe.Fori(1, groups - 1) as g:
                    tensor_group(pe, g, False, False)
                tensor_group(pe, groups - 1, False, True)


def build(nc, d):
    with ExitStack() as ctx:
        sb = lambda name, shape, dt: ctx.enter_context(nc.sbuf_tensor(name, shape, dt))
        keep = {
            "ident": sb("ident", [P, P], F32),
            "gu_vals": sb("gu_vals", [P, GU, 2, T // 2], BF16),
            "dn_vals": sb("dn_vals", [P, KT, 2, INNER // 2], BF16),
            "gu_sc": sb("gu_sc", [P, KT, GU], F32),
            "dn_sc": sb("dn_sc", [P, IT, KT], F32),
            "gates": sb("gates", [P, 2], F32),
            "qk_dram": nc.dram_tensor("qk_scratch", [B, 2, HEADS, KC, 2, T], F32).ap(),
            "x_dram": nc.dram_tensor("x_scratch", [B, P, T], F32).ap(),
        }
        attend(nc, d, keep)
        keep.update({
            "gu_head": sb("gu_head", [P, KT, 2 * INNER], F32R),
            "gu_rest": sb("gu_rest", [P, KT, 2 * INNER], BF16),
            "dn_head": sb("dn_head", [P, IT, T], F32R),
            "dn_rest": sb("dn_rest", [P, IT, T], BF16),
        })
        feed_forward(nc, d, keep)


def kernel(**inputs):
    import concourse.bacc as bacc
    from concourse.bass_utils import run_bass_kernel_spmd

    a = {k: np.ascontiguousarray(v) for k, v in inputs.items()}
    theta = (1.0 / np.float32(10000.0) ** (np.arange(0, ROT, 2, dtype=np.float32) / np.float32(ROT))).astype(np.float32)
    angle = np.arange(T, dtype=np.float32)[None, :] * np.concatenate([theta, theta])[:, None]
    turn = np.concatenate([-np.ones(ROT // 2, np.float32), np.ones(ROT // 2, np.float32)])[:, None]
    cos, sin = np.cos(angle), np.sin(angle) * turn
    order = np.arange(P).reshape(HEADS, 2, ROT).transpose(1, 0, 2).reshape(P)
    bq, bk = (a[n][order].reshape(2, P // 2) for n in ("L0_xattn_bq", "L0_xattn_bk"))
    arrays = {
        "x": a["x"], "ctx": a["ctx_2048"], "g_xattn": a["g_xattn"], "g_ffn": a["g_ffn"],
        "wqT": np.ascontiguousarray(a["L0_xattn_Wq"][order].T), "wkT": np.ascontiguousarray(a["L0_xattn_Wk"][order].T),
        "wvT": np.ascontiguousarray(a["L0_xattn_Wv"].T), "woT": np.ascontiguousarray(a["L0_xattn_Wo"].T),
        "qk_bias": np.ascontiguousarray(np.concatenate([bq, bk], axis=1).T), "bv": a["L0_xattn_bv"], "bo": a["L0_xattn_bo"],
        "gate_up_packed": a["L0_ffn_gate_up_packed"].view(np.uint32), "gate_up_scales": a["L0_ffn_gate_up_scales"],
        "down_packed": a["L0_ffn_down_packed"].view(np.uint32), "down_scales": a["L0_ffn_down_scales"],
        "cos": np.tile(cos, (2 * HEADS, 1)).astype(np.float32), "sin": np.tile(sin, (2 * HEADS, 1)).astype(np.float32),
        "ident": np.eye(P, dtype=np.float32),
    }
    nc = bacc.Bacc("TRN2", target_bir_lowering=False, num_devices=1)
    d = {name: nc.dram_tensor(name + "_dram", v.shape, mybir.dt.from_np(v.dtype), kind="ExternalInput").ap()
         for name, v in arrays.items()}
    d["out"] = nc.dram_tensor("out_dram", (B, P, T), F32, kind="ExternalOutput").ap()
    build(nc, d)
    r = run_bass_kernel_spmd(nc, [{name + "_dram": v for name, v in arrays.items()}], core_ids=[0])
    return r.results[0]["out_dram"]
```
